# Optimizing a Trainium2 kernel written in Bass

```python
import numpy as np
import jax
import jax.numpy as jnp

def _softmax(x, axis=-1):
    return jax.nn.softmax(x, axis=axis)

def _gelu(x):
    return jax.nn.gelu(x, approximate=True)

def _silu(x):
    return jax.nn.silu(x)

def _sigmoid(x):
    return jax.nn.sigmoid(x)

def _layernorm(x, axis=-1, eps=1e-05):
    m = jnp.mean(x, axis=axis, keepdims=True)
    v = jnp.var(x, axis=axis, keepdims=True)
    return (x - m) / jnp.sqrt(v + eps)

def _scatter_add(tgt, idx, src, axis=0):
    return tgt.at[idx].add(src)

def _segment_sum(src, seg, n):
    return jax.ops.segment_sum(src, seg, n)
kernel_name = 'mk_gps_d1_gnn_r8_43d074'

def setup_inputs(seed: int=0):
    np.random.seed(seed)
    _w = jnp.asarray

    def _rec_inputs():
        import jax
        import jax.numpy as jnp
        _gk = jax.random.key(seed)
        x = -0.0003713 + 1 * jax.random.normal(jax.random.fold_in(_gk, 1), (12500, 256), jnp.float32)
        src = jax.random.randint(jax.random.fold_in(_gk, 2), (200000,), 0, 12500, jnp.int32)
        dst = jax.random.randint(jax.random.fold_in(_gk, 3), (200000,), 0, 12500, jnp.int32)
        _o = jnp.argsort(dst, stable=True)
        src = src[_o]
        dst = dst[_o]
        edge_weight1 = 0.000937891 + 0.999965 * jax.random.normal(jax.random.fold_in(_gk, 13), (200000, 1), jnp.float32)
        return (x, src, dst, edge_weight1)
    x, src, dst, edge_weight1 = _rec_inputs()

    def _L0_gnn_setup():
        import jax, jax.numpy as jnp
        import numpy as np
        N, E, IN_DIM, HEADS, OUT_DIM, N_GRAPHS = (6250, 100000, 256, 4, 64, 8)
        HC = HEADS * OUT_DIM
        NEG_SLOPE = 0.2
        LN_EPS = 1e-05
        key = jax.random.key(seed)
        ks = jax.random.split(key, 12)
        x = jax.random.normal(ks[0], (N, IN_DIM), jnp.float32)
        edge_attr = jax.random.normal(ks[1], (E, 1), jnp.float32)
        src = jax.random.randint(ks[2], (E,), 0, N, dtype=jnp.int32)
        dst = jax.random.randint(ks[3], (E,), 0, N, dtype=jnp.int32)
        edge_index = jnp.stack([src, dst]).astype(jnp.int64)
        batch = jnp.sort(jax.random.randint(ks[4], (N,), 0, N_GRAPHS, dtype=jnp.int32)).astype(jnp.int64)
        s = 1.0 / np.sqrt(IN_DIM)
        W_src = jax.random.uniform(ks[5], (IN_DIM, HC), jnp.float32, -s, s)
        W_dst = jax.random.uniform(ks[6], (IN_DIM, HC), jnp.float32, -s, s)
        att_src = jax.random.uniform(ks[7], (HEADS, OUT_DIM), jnp.float32, -s, s)
        att_dst = jax.random.uniform(ks[8], (HEADS, OUT_DIM), jnp.float32, -s, s)
        bias = jnp.zeros((HC,), jnp.float32)
        ln_gamma = jnp.ones((HC,), jnp.float32)
        ln_beta = jnp.zeros((HC,), jnp.float32)
        prelu_w = jnp.full((HC,), 0.25, jnp.float32)
        return {'x': x, 'edge_attr': edge_attr, 'W_src': W_src, 'W_dst': W_dst, 'att_src': att_src, 'att_dst': att_dst, 'bias': bias, 'ln_gamma': ln_gamma, 'ln_beta': ln_beta, 'prelu_w': prelu_w, 'edge_index': edge_index, 'batch': batch}
    _L0_gnn_all = _L0_gnn_setup()
    _L0_gnn_in = {k: v for k, v in _L0_gnn_all.items() if k in ('W_src', 'W_dst', 'att_src', 'att_dst', 'bias', 'ln_gamma', 'ln_beta', 'prelu_w')}
    del _L0_gnn_all

    def _L0_mix_setup():
        import jax, jax.numpy as jnp
        import numpy as np
        NHEAD = 8
        ATT_EPS = 1e-06
        LN_EPS = 1e-05

        def _layernorm(x, g, b):
            mu = jnp.mean(x, axis=-1, keepdims=True)
            var = jnp.mean(jnp.square(x - mu), axis=-1, keepdims=True)
            return (x - mu) * jax.lax.rsqrt(var + LN_EPS) * g + b
        key = jax.random.key(seed)
        ks = jax.random.split(key, 7)
        N, L, C = (4, 2048, 256)
        s = 1.0 / np.sqrt(C)
        return {'x': jax.random.normal(ks[0], (N, L, C), jnp.float32), 'Wq': jax.random.normal(ks[1], (C, C), jnp.float32) * s, 'Wk': jax.random.normal(ks[2], (C, C), jnp.float32) * s, 'Wv': jax.random.normal(ks[3], (C, C), jnp.float32) * s, 'Wm': jax.random.normal(ks[4], (C, C), jnp.float32) * s, 'W1': jax.random.normal(ks[5], (2 * C, 2 * C), jnp.float32) * (1.0 / np.sqrt(2 * C)), 'W2': jax.random.normal(ks[6], (2 * C, C), jnp.float32) * (1.0 / np.sqrt(2 * C)), 'g1': jnp.ones((C,), jnp.float32), 'b1': jnp.zeros((C,), jnp.float32), 'g2': jnp.ones((C,), jnp.float32), 'b2': jnp.zeros((C,), jnp.float32)}
    _L0_mix_all = _L0_mix_setup()
    _L0_mix_in = {k: v for k, v in _L0_mix_all.items() if k in ('Wq', 'Wk', 'Wv', 'Wm', 'W1', 'W2', 'g1', 'b1', 'g2', 'b2')}
    del _L0_mix_all

    def _L0_ffn_setup():
        import jax, jax.numpy as jnp
        import numpy as np
        BN_EPS = 0.001

        def _bn(h, g, b, m, v):
            return g * (h - m) * jax.lax.rsqrt(v + BN_EPS) + b
        key = jax.random.key(seed)
        ks = jax.random.split(key, 8)
        B, F, Df = (256, 64, 256)
        E, H, D = (8, 256, 256)
        s1 = 1.0 / np.sqrt(Df)
        s2 = 1.0 / np.sqrt(H)
        return {'x': jax.random.normal(ks[0], (B, F, Df), jnp.float32), 'Wr': jax.random.normal(ks[1], (Df, E), jnp.float32) * s1, 'br': jnp.zeros((E,), jnp.float32), 'W1': jax.random.normal(ks[2], (E, Df, H), jnp.float32) * s1, 'b1': jnp.zeros((E, H), jnp.float32), 'g1': jnp.ones((E, H), jnp.float32), 'be1': jnp.zeros((E, H), jnp.float32), 'm1': jnp.zeros((E, H), jnp.float32), 'v1': jnp.ones((E, H), jnp.float32), 'W2': jax.random.normal(ks[3], (E, H, H), jnp.float32) * s2, 'b2': jnp.zeros((E, H), jnp.float32), 'g2': jnp.ones((E, H), jnp.float32), 'be2': jnp.zeros((E, H), jnp.float32), 'm2': jnp.zeros((E, H), jnp.float32), 'v2': jnp.ones((E, H), jnp.float32), 'Wo': jax.random.normal(ks[4], (E, H, D), jnp.float32) * s2, 'bo': jnp.zeros((E, D), jnp.float32)}
    _L0_ffn_all = _L0_ffn_setup()
    _L0_ffn_in = {k: v for k, v in _L0_ffn_all.items() if k in ('Wr', 'br', 'W1', 'b1', 'g1', 'be1', 'm1', 'v1', 'W2', 'b2', 'g2', 'be2', 'm2', 'v2', 'Wo', 'bo')}
    del _L0_ffn_all
    return {'x': x, 'src': src, 'dst': dst, 'edge_weight1': edge_weight1, 'L0_gnn_W_src': _L0_gnn_in['W_src'], 'L0_gnn_W_dst': _L0_gnn_in['W_dst'], 'L0_gnn_att_src': _L0_gnn_in['att_src'], 'L0_gnn_att_dst': _L0_gnn_in['att_dst'], 'L0_gnn_bias': _L0_gnn_in['bias'], 'L0_gnn_ln_gamma': _L0_gnn_in['ln_gamma'], 'L0_gnn_ln_beta': _L0_gnn_in['ln_beta'], 'L0_gnn_prelu_w': _L0_gnn_in['prelu_w'], 'L0_mix_Wq': _L0_mix_in['Wq'], 'L0_mix_Wk': _L0_mix_in['Wk'], 'L0_mix_Wv': _L0_mix_in['Wv'], 'L0_mix_Wm': _L0_mix_in['Wm'], 'L0_mix_W1': _L0_mix_in['W1'], 'L0_mix_W2': _L0_mix_in['W2'], 'L0_mix_g1': _L0_mix_in['g1'], 'L0_mix_b1': _L0_mix_in['b1'], 'L0_mix_g2': _L0_mix_in['g2'], 'L0_mix_b2': _L0_mix_in['b2'], 'L0_ffn_Wr': _L0_ffn_in['Wr'], 'L0_ffn_br': _L0_ffn_in['br'], 'L0_ffn_W1': _L0_ffn_in['W1'], 'L0_ffn_b1': _L0_ffn_in['b1'], 'L0_ffn_g1': _L0_ffn_in['g1'], 'L0_ffn_be1': _L0_ffn_in['be1'], 'L0_ffn_m1': _L0_ffn_in['m1'], 'L0_ffn_v1': _L0_ffn_in['v1'], 'L0_ffn_W2': _L0_ffn_in['W2'], 'L0_ffn_b2': _L0_ffn_in['b2'], 'L0_ffn_g2': _L0_ffn_in['g2'], 'L0_ffn_be2': _L0_ffn_in['be2'], 'L0_ffn_m2': _L0_ffn_in['m2'], 'L0_ffn_v2': _L0_ffn_in['v2'], 'L0_ffn_Wo': _L0_ffn_in['Wo'], 'L0_ffn_bo': _L0_ffn_in['bo']}

def reference(x, src, dst, edge_weight1, L0_gnn_W_src, L0_gnn_W_dst, L0_gnn_att_src, L0_gnn_att_dst, L0_gnn_bias, L0_gnn_ln_gamma, L0_gnn_ln_beta, L0_gnn_prelu_w, L0_mix_Wq, L0_mix_Wk, L0_mix_Wv, L0_mix_Wm, L0_mix_W1, L0_mix_W2, L0_mix_g1, L0_mix_b1, L0_mix_g2, L0_mix_b2, L0_ffn_Wr, L0_ffn_br, L0_ffn_W1, L0_ffn_b1, L0_ffn_g1, L0_ffn_be1, L0_ffn_m1, L0_ffn_v1, L0_ffn_W2, L0_ffn_b2, L0_ffn_g2, L0_ffn_be2, L0_ffn_m2, L0_ffn_v2, L0_ffn_Wo, L0_ffn_bo):
    import jax
    import jax.numpy as jnp

    def _L0_gnn_ref(x, edge_attr, W_src, W_dst, att_src, att_dst, bias, ln_gamma, ln_beta, prelu_w, edge_index, batch):
        import jax, jax.numpy as jnp
        import numpy as np
        N, E, IN_DIM, HEADS, OUT_DIM, N_GRAPHS = (6250, 100000, 256, 4, 64, 8)
        HC = HEADS * OUT_DIM
        NEG_SLOPE = 0.2
        LN_EPS = 1e-05
        src, dst = (edge_index[0], edge_index[1])
        n = x.shape[0]
        h_src = (x @ W_src).reshape(n, HEADS, OUT_DIM)
        h_dst = (x @ W_dst).reshape(n, HEADS, OUT_DIM)
        a_src = jnp.einsum('nhc,hc->nh', h_src, att_src)
        a_dst = jnp.einsum('nhc,hc->nh', h_dst, att_dst)
        e = a_src[src] + a_dst[dst]
        e = jnp.where(e > 0, e, NEG_SLOPE * e)
        m = jax.ops.segment_max(e, dst, num_segments=n)
        p = jnp.exp(e - m[dst])
        denom = jax.ops.segment_sum(p, dst, num_segments=n)
        alpha = p / jnp.maximum(denom[dst], 1e-16)
        msg = alpha[:, :, None] * h_src[src]
        out = jax.ops.segment_sum(msg, dst, num_segments=n).reshape(n, HC) + bias
        mu = out.mean(-1, keepdims=True)
        var = ((out - mu) ** 2).mean(-1, keepdims=True)
        out = (out - mu) * jax.lax.rsqrt(var + LN_EPS) * ln_gamma + ln_beta
        return jnp.where(out > 0, out, prelu_w * out)

    def _L0_mix_ref(x, Wq, Wk, Wv, Wm, W1, W2, g1, b1, g2, b2):
        import jax, jax.numpy as jnp
        import numpy as np
        NHEAD = 8
        ATT_EPS = 1e-06
        LN_EPS = 1e-05

        def _layernorm(x, g, b):
            mu = jnp.mean(x, axis=-1, keepdims=True)
            var = jnp.mean(jnp.square(x - mu), axis=-1, keepdims=True)
            return (x - mu) * jax.lax.rsqrt(var + LN_EPS) * g + b
        N, L, C = x.shape
        H = NHEAD
        D = C // H
        q = (x @ Wq).reshape(N, L, H, D)
        k = (x @ Wk).reshape(N, L, H, D)
        v = (x @ Wv).reshape(N, L, H, D)
        Q = jax.nn.elu(q) + 1.0
        K = jax.nn.elu(k) + 1.0
        v = v / L
        KV = jnp.einsum('nshd,nshv->nhdv', K, v)
        Z = 1.0 / (jnp.einsum('nlhd,nhd->nlh', Q, K.sum(axis=1)) + ATT_EPS)
        msg = jnp.einsum('nlhd,nhdv,nlh->nlhv', Q, KV, Z) * L
        msg = msg.reshape(N, L, C) @ Wm
        msg = _layernorm(msg, g1, b1)
        h = jnp.concatenate([x, msg], axis=-1) @ W1
        h = jax.nn.relu(h) @ W2
        msg = _layernorm(h, g2, b2)
        return x + msg

    def _L0_ffn_ref(x, Wr, br, W1, b1, g1, be1, m1, v1, W2, b2, g2, be2, m2, v2, Wo, bo):
        import jax, jax.numpy as jnp
        import numpy as np
        BN_EPS = 0.001

        def _bn(h, g, b, m, v):
            return g * (h - m) * jax.lax.rsqrt(v + BN_EPS) + b
        feat = jnp.mean(x, axis=0)
        w = jax.nn.softmax(feat @ Wr + br, axis=-1)
        h = jnp.einsum('bfd,edh->bfeh', x, W1) + b1
        h = jax.nn.relu(_bn(h, g1, be1, m1, v1))
        h = jnp.einsum('bfeh,ehk->bfek', h, W2) + b2
        h = jax.nn.relu(_bn(h, g2, be2, m2, v2))
        y = jnp.einsum('bfeh,ehd->bfed', h, Wo) + bo
        return jnp.einsum('bfed,fe->bfd', y, w)
    edge_index = jnp.stack([src, dst])
    batch0 = jnp.zeros((12500,), jnp.int32)
    xn = _layernorm(x, axis=-1)
    x = x + _L0_gnn_ref(xn, edge_weight1, L0_gnn_W_src, L0_gnn_W_dst, L0_gnn_att_src, L0_gnn_att_dst, L0_gnn_bias, L0_gnn_ln_gamma, L0_gnn_ln_beta, L0_gnn_prelu_w, edge_index, batch0) + _L0_mix_ref(xn[None], L0_mix_Wq, L0_mix_Wk, L0_mix_Wv, L0_mix_Wm, L0_mix_W1, L0_mix_W2, L0_mix_g1, L0_mix_b1, L0_mix_g2, L0_mix_b2)[0]
    x = x + _L0_ffn_ref(_layernorm(x, axis=-1)[None], L0_ffn_Wr, L0_ffn_br, L0_ffn_W1, L0_ffn_b1, L0_ffn_g1, L0_ffn_be1, L0_ffn_m1, L0_ffn_v1, L0_ffn_W2, L0_ffn_b2, L0_ffn_g2, L0_ffn_be2, L0_ffn_m2, L0_ffn_v2, L0_ffn_Wo, L0_ffn_bo)[0]
    return x

_drawn_inputs = setup_inputs


def setup_inputs(seed=0):
    import zlib

    import numpy as np

    out = dict(_drawn_inputs(seed))
    spreads = {'L0_gnn_bias': (0.0, 0.1),
     'L0_gnn_ln_gamma': (1.0, 0.2),
     'L0_gnn_ln_beta': (0.0, 0.1),
     'L0_gnn_prelu_w': (0.25, 0.6),
     'L0_mix_g1': (1.0, 0.2),
     'L0_mix_b1': (0.0, 0.274),
     'L0_mix_g2': (1.0, 0.2),
     'L0_mix_b2': (0.0, 0.1),
     'L0_ffn_br': (0.0, 0.573),
     'L0_ffn_b1': (0.0, 0.732),
     'L0_ffn_g1': (1.0, 0.6),
     'L0_ffn_be1': (0.0, 0.746),
     'L0_ffn_m1': (0.0, 0.737),
     'L0_ffn_v1': (1.0, 0.6),
     'L0_ffn_b2': (0.0, 0.514),
     'L0_ffn_g2': (1.0, 0.6),
     'L0_ffn_be2': (0.0, 0.564),
     'L0_ffn_m2': (0.0, 0.539),
     'L0_ffn_v2': (1.0, 0.6),
     'L0_ffn_bo': (0.0, 0.388)}
    factors = {'L0_gnn_W_dst': 13.95, 'L0_gnn_att_dst': 14.219}
    for name, (base, spread) in spreads.items():
        noise = np.random.default_rng([zlib.crc32(name.encode()), seed]).standard_normal(out[name].shape)
        drawn = base * np.exp(spread * noise) if base else spread * noise
        out[name] = jnp.asarray(drawn.astype(out[name].dtype))
    for name, factor in factors.items():
        out[name] = (out[name] * factor).astype(out[name].dtype)
    return out
```

```python
import numpy as np
import concourse.bass as bass
from concourse import mybir
from contextlib import ExitStack

P = 128
D = 256
HEADS = 4
KD = D // P
CH = 4
CT = CH * P
NEXP = 8
ATT_D = 32
BIG = 1.0e30
GU = 4
GB = 16
MW = D + HEADS
RECW = 10
LN_EPS = 1e-5
BN_EPS = 1e-3
ATT_EPS = 1e-6
MAGIC = 1597463007.0

C_H, C_AS, C_AD, C_K, C_V, C_END = 0, 256, 260, 264, 520, 776
R_BIAS, R_GAMMA, R_BETA, R_PRELU, R_G2, R_B2, R_BR, R_ATS, R_ATD, R_END = 0, 256, 512, 768, 1024, 1280, 1536, 1544, 1800, 2056
Q_B1, Q_G1, Q_BE1, Q_M1, Q_V1, Q_B2, Q_G2, Q_BE2, Q_M2, Q_V2, Q_MG, Q_MB, Q_END = [16 * i for i in range(11)] + [162, 164]


def ring(eng, total, slots, body, ahead=1):
    rounds = (total - ahead) // slots
    if rounds < 2:
        rounds = 1 if total > slots else 0
    for c in range(min(slots, total)):
        body(c, c, 0, c == total - 1)
    if rounds > 1:
        with eng.Fori(1, rounds) as i:
            for s in range(slots):
                body(i * slots + s, s, i, False)
    for c in range(max(rounds, 1) * slots, total):
        body(c, c % slots, c // slots, c == total - 1)


def used(eng, sem, per, n):
    if not (isinstance(n, int) and n == 0):
        eng.wait_ge(sem, per * n)


class Stage:

    def __init__(self, sem, per=1):
        self.sem, self.per = sem, per

    def wait(self, eng, turn, k=None):
        if not (isinstance(turn, int) and turn < 0):
            eng.wait_ge(self.sem, turn * self.per + (self.per if k is None else k))


def build(nc, a, out, N, E):
    f32, i32, bf16 = mybir.dt.float32, mybir.dt.int32, mybir.dt.bfloat16
    ALU, ACT, AX = mybir.AluOpType, mybir.ActivationFunctionType, mybir.AxisListType
    ET = mybir.EngineType

    NP = -(-N // CT) * CT
    NT, NCH = NP // P, NP // CT
    EP = -(-E // (P * GB)) * P * GB
    W = EP // P
    TE = W
    NB = -(-(TE + NT - 1) // GU)
    STEPS = NB * GU
    assert STEPS <= TE + NT
    KC = a["last_dst"].shape[1]
    NBLK = W // GB

    es = ExitStack()
    with es:
        def sb(name, shape, dt=f32):
            return es.enter_context(nc.sbuf_tensor(name, shape, dt))

        def sem(name):
            return es.enter_context(nc.semaphore(name))

        def dram(name, shape):
            return nc.dram_tensor(name, shape, f32, kind="Internal").ap()

        def stage(name, per=1):
            return Stage(sem(name), per)

        passed = {e: sem(f"passed_{e}") for e in ("sp", "dve", "pool")}

        def pass_on(eng, name):
            eng.sem_inc(passed[name], 1)

        class Region:
            def __init__(self, t):
                self.t, self.at = t, 0

            def take(self, *dims, dt=f32, parts=P):
                n = int(np.prod(dims))
                v = self.t[0:parts, self.at:self.at + n]
                self.at += -(-n // 8) * 8
                assert self.at <= self.t.shape[1], (self.at, self.t.shape)
                if dt != f32:
                    v = v.bitcast(dt)
                if len(dims) == 2:
                    v = v.rearrange("p (a b) -> p a b", b=dims[1])
                if len(dims) == 3:
                    v = v.rearrange("p (a b c) -> p a b c", b=dims[1], c=dims[2])
                return v

        h_tab = dram("h_tab", (NP, D))
        as_tab = dram("as_tab", (NP, HEADS))
        ad_tab = dram("ad_tab", (NP, HEADS))
        xnt_tab = dram("xnt_tab", (P, KD, NP))
        base_tab = dram("base_tab", (NP, D))
        rec_tab = dram("rec_tab", ((TE + 1) * P, RECW))

        ident = sb("ident", [P, P])
        iota_row = sb("iota_row", [P, P])
        rows = sb("rows", [P, R_END])
        cols = sb("cols", [P, Q_END])
        wr = sb("wr", [P, KD * NEXP])[:, :].rearrange("p (k e) -> p k e", k=KD)
        bo = sb("bo", [NEXP, D])
        acc_t = sb("acc", [P, max(NT * MW, 25000)])
        wf_t = sb("wf", [P, 3 * NEXP * KD * D])
        work_t = sb("work", [P, 12088])
        bn = sb("bn", [P, 4 * 16])
        acc = acc_t[:, 0:NT * MW].rearrange("p (j c) -> p j c", c=MW)

        ps = [es.enter_context(nc.psum_tensor(f"ps{i}", [P, 512], f32)) for i in range(8)]

        def row(at, n=D):
            return rows[:, at:at + n]

        def rsqrt(dve, st, turn, k, y, v, vv, t, eps):
            def link(ins):
                nonlocal k
                k += 1
                ins.then_inc(st.sem, 1)
                st.wait(dve, turn, k)
            link(nc.vector.tensor_scalar(vv, v, 1.0, eps, ALU.mult, ALU.add))
            link(nc.vector.tensor_scalar(t.bitcast(i32), vv.bitcast(i32), 1, None, ALU.logical_shift_right))
            link(nc.vector.tensor_scalar(y.bitcast(i32), t.bitcast(i32), -1.0, MAGIC, ALU.mult, ALU.add))
            for _ in range(3):
                link(nc.vector.tensor_tensor(t, y, y, ALU.mult))
                link(nc.vector.scalar_tensor_tensor(t, t, -0.5, vv, ALU.mult, ALU.mult))
                link(nc.vector.scalar_tensor_tensor(y, t, 1.5, y, ALU.add, ALU.mult))
            return k

        RSQ = 12

        r1 = Region(acc_t)
        kvbd = r1.take(KD, P)
        ksbd = r1.take(KD, P)
        wq = r1.take(KD, D)
        wm = r1.take(KD, D)
        w1 = r1.take(2 * KD, 2 * D)
        w2 = r1.take(2 * KD, D)
        r2_from = r1.at
        wcat = r1.take(KD, C_END)
        wdst = r1.take(KD, D)
        fold = r1.take(2, KD, D)
        X = [r1.take(CH, D) for _ in range(2)]
        XN = [r1.take(CH, D) for _ in range(2)]
        XB = [r1.take(CH, D) for _ in range(2)]
        XT = [r1.take(KD, CT) for _ in range(2)]
        HS = [r1.take(CH, C_K) for _ in range(2)]
        KE = r1.take(CH, D)
        KR = r1.take(CH, D)
        KK = r1.take(CH, D)
        VX = r1.take(CH, KD, P + 1)
        zeros = r1.take(2 * (P + 1))
        stats = r1.take(CH, 6)
        mv = r1.take(CH, 2)
        rstd = r1.take(CH)
        tv = r1.take(CH)
        tt = r1.take(CH)
        p_kv = ps[6][:, 0:2 * (P + 1)].rearrange("p (g c) -> p g c", g=2)

        par_in, w_in, id_set, ones_set = sem("par_in"), sem("w_in"), sem("id_set"), sem("ones_set")
        fold_mul, fold_sum, id_zero = sem("fold_mul"), sem("fold_sum"), sem("id_zero")
        x_in = [sem(f"x_in{s}") for s in range(2)]
        x_stat, x_aggr, x_rs, x_norm, x_base = (stage("x_stat"), stage("x_aggr"), stage("x_rs", RSQ), stage("x_norm"),
                                                stage("x_base"))
        x_tr, xt_ev = stage("x_tr", 2), stage("xt_ev", 2)
        hk_mm, h_ev, k_act, k_dve, v_ev, kv_mm = (stage("hk_mm", CH), stage("h_ev", CH), stage("k_act", CH),
                                                  stage("k_dve", CH), stage("v_ev", CH), stage("kv_mm", CH))
        st_h = [sem(f"st_h{s}") for s in range(2)]
        kv_zero, kv_all, kv_cp = sem("kv_zero"), sem("kv_all"), sem("kv_cp")
        x_v = a["x"].rearrange("(c t p) d -> c p t d", t=CH, p=P)
        base_v = base_tab.rearrange("(c t p) d -> c p t d", t=CH, p=P)
        h_v = h_tab.rearrange("(c t p) d -> c p t d", t=CH, p=P)
        as_v = as_tab.rearrange("(c t p) d -> c p t d", t=CH, p=P)
        ad_v = ad_tab.rearrange("(c t p) d -> c p t d", t=CH, p=P)
        xnt_v = xnt_tab.rearrange("p k (c n) -> c p k n", n=CT)
        out_v = out.rearrange("(c t p) d -> c p t d", t=CH, p=P)

        def at(view, c):
            if isinstance(c, int):
                return view[c]
            return view[bass.ds(c, 1)].rearrange("o p k n -> (o p) k n")

        def weight(name):
            return a[name].rearrange("(k p) n -> p k n", p=P)

        with nc.Block() as block:
            @block.sync
            def _(sp):
                sp.dma_start(wcat[:, :, C_H:C_AS], weight("L0_gnn_W_src")).then_inc(w_in, 16)
                sp.dma_start(wdst, weight("L0_gnn_W_dst")).then_inc(w_in, 16)
                sp.dma_start(X[0], x_v[0]).then_inc(x_in[0], 16)
                sp.dma_start(rows[:, :], a["rows"]).then_inc(w_in, 16)
                sp.dma_start(wcat[:, :, C_K:C_V], weight("L0_mix_Wk")).then_inc(w_in, 16)
                sp.dma_start(wcat[:, :, C_V:C_END], weight("L0_mix_Wv")).then_inc(w_in, 16)
                for dst, src in ((cols[:, :], a["cols"]), (wr, weight("L0_ffn_Wr")), (bo[:, :], a["L0_ffn_bo"]),
                                 (wq, weight("L0_mix_Wq")), (wm, weight("L0_mix_Wm")), (w1, weight("L0_mix_W1")),
                                 (w2, weight("L0_mix_W2"))):
                    sp.dma_start(dst, src).then_inc(par_in, 16)

                def body(c, s, n, last):
                    if not last:
                        x_base.wait(sp, c - 1)
                        pass_on(sp, "sp")
                        sp.dma_start(X[1 - s], at(x_v, c + 1)).then_inc(x_in[1 - s], 16)
                    x_base.wait(sp, c)
                    pass_on(sp, "sp")
                    sp.dma_start(at(base_v, c), XB[s]).then_inc(st_h[s], 16)
                    xt_ev.wait(sp, c)
                    pass_on(sp, "sp")
                    sp.dma_start(at(xnt_v, c), XT[s]).then_inc(st_h[s], 16)
                    h_ev.wait(sp, c)
                    pass_on(sp, "sp")
                    sp.dma_start(at(h_v, c), HS[s][:, :, 0:D]).then_inc(st_h[s], 16)
                    sp.dma_start(at(as_v, c), HS[s][:, :, C_AS:C_AD]).then_inc(st_h[s], 16)
                    sp.dma_start(at(ad_v, c), HS[s][:, :, C_AD:C_K]).then_inc(st_h[s], 16)
                ring(sp, NCH, 2, body)
                sp.wait_ge(st_h[0], 80 * ((NCH + 1) // 2))
                sp.wait_ge(st_h[1], 80 * (NCH // 2))
                sp.wait_ge(par_in, 16 * 7)

            @block.gpsimd
            def _(pool):
                nc.gpsimd.memset(ident[:, :], 0.0).then_inc(id_zero, 1)
                nc.gpsimd.iota(iota_row[:, :], pattern=[[1, P]], base=0, channel_multiplier=0,
                               allow_small_or_imprecise_dtypes=True)
                nc.gpsimd.memset(VX[:, :, :, P:P + 1], 1.0)
                nc.gpsimd.memset(zeros, 0.0).then_inc(ones_set, 1)
                pool.wait_ge(id_zero, 1)
                nc.gpsimd.affine_select(out=ident[:, :], in_=ident[:, :], compare_op=ALU.not_equal, fill=1.0, base=0,
                                        pattern=[[-1, P]], channel_multiplier=1).then_inc(id_set, 1)

            @block.vector
            def _(dve):
                dve.wait_ge(w_in, 80)
                for j, (w, r) in enumerate(((wcat[:, :, C_H:C_AS], R_ATS), (wdst, R_ATD))):
                    nc.vector.tensor_tensor(fold[:, j], w, row(r).unsqueeze(1).broadcast_to([P, KD, D]),
                                            ALU.mult).then_inc(fold_mul, 1)
                dve.wait_ge(fold_mul, 2)
                for j, col in enumerate((C_AS, C_AD)):
                    for k in range(KD):
                        nc.vector.tensor_reduce(wcat[:, k, col:col + HEADS],
                                                fold[:, j, k].rearrange("p (h c) -> p h c", h=HEADS), AX.X,
                                                ALU.add).then_inc(fold_sum, 1)

                def body(c, s, n, last):
                    dve.wait_ge(x_in[s], 16 * (n + 1))
                    for t in range(CH):
                        ins = nc.vector.bn_stats(stats[:, t], X[s][:, t])
                    ins.then_inc(x_stat.sem, 1)
                    x_stat.wait(dve, c)
                    pass_on(dve, "dve")
                    for t in range(CH):
                        ins = nc.vector.bn_aggr(mv[:, t], stats[:, t])
                    ins.then_inc(x_aggr.sem, 1)
                    x_aggr.wait(dve, c)
                    rsqrt(dve, x_rs, c, 0, rstd, mv[:, :, 1], tv, tt, LN_EPS)
                    for t in range(CH):
                        ins = nc.vector.tensor_scalar(XN[s][:, t], X[s][:, t], mv[:, t, 0:1], rstd[:, t:t + 1],
                                                      ALU.subtract, ALU.mult)
                    ins.then_inc(x_norm.sem, 1)
                    x_norm.wait(dve, c)
                    used(dve, st_h[s], 80, n)
                    nc.vector.tensor_tensor(XB[s], X[s], XN[s], ALU.add).then_inc(x_base.sem, 1)
                    for t in range(CH):
                        k_act.wait(dve, c, t + 1)
                        kv_mm.wait(dve, c - 1, t + 1)
                        nc.vector.scalar_tensor_tensor(KK[:, t], KE[:, t], 1.0, KR[:, t], ALU.min,
                                                       ALU.add).then_inc(k_dve.sem, 1)
                        nc.vector.tensor_copy(VX[:, t, :, 0:P],
                                              ps[4 + t % 2][:, D:2 * D].rearrange("p (g c) -> p g c", g=KD)
                                              ).then_inc(v_ev.sem, 1)
                ring(dve, NCH, 2, body)
                dve.wait_ge(id_set, 1)
                nc.vector.memset(kvbd, 0.0)
                nc.vector.memset(ksbd, 0.0).then_inc(kv_cp, 1)
                dve.wait_ge(kv_cp, 1)
                dve.wait_ge(kv_all, 1)
                for g in range(KD):
                    for b in range(P // ATT_D):
                        o = slice(b * ATT_D, (b + 1) * ATT_D)
                        nc.vector.tensor_copy(kvbd[o, g, o], p_kv[o, g, o])
                        nc.vector.tensor_copy(ksbd[o, g, o], p_kv[o, g, P:P + 1].broadcast_to([ATT_D, ATT_D])
                                              ).then_inc(kv_cp, 1)

            @block.scalar
            def _(act):

                def body(c, s, n, last):
                    used(act, st_h[s], 80, n)
                    hk_mm.wait(act, c - 1)
                    for k in range(KD):
                        x_tr.wait(act, c, k + 1)
                        nc.scalar.activation(XT[s][:, k], ps[k][:, :], ACT.Copy).then_inc(xt_ev.sem, 1)
                    for t in range(CH):
                        hk_mm.wait(act, c, t + 1)
                        nc.scalar.activation(HS[s][:, t], ps[2 + t % 2][:, 0:C_K], ACT.Copy).then_inc(h_ev.sem, 1)
                        k_dve.wait(act, c - 1, t + 1)
                        nc.scalar.activation(KE[:, t], ps[4 + t % 2][:, 0:D], ACT.Exp)
                        nc.scalar.activation(KR[:, t], ps[4 + t % 2][:, 0:D], ACT.Relu).then_inc(k_act.sem, 1)
                ring(act, NCH, 2, body)

            @block.tensor
            def _(pe):
                pe.wait_ge(ones_set, 1)
                pe.wait_ge(id_set, 1)
                pe.wait_ge(fold_sum, 4)
                nc.tensor.matmul(ps[6][:, 0:2 * (P + 1)], zeros[:, 0:P], zeros, start=True, stop=False)

                def kv_sum(c, t, last):
                    k_dve.wait(pe, c, t + 1)
                    v_ev.wait(pe, c, t + 1)
                    rows_in = P if not last else min(P, N - (c * CH + t) * P)
                    final = last and N - (c * CH + t + 1) * P <= 0
                    if rows_in <= 0:
                        nc.tensor.matmul(ps[7][:, 0:64], zeros[:, 0:P], zeros[:, 0:64], start=True,
                                         stop=True).then_inc(kv_mm.sem, 1)
                        return
                    for g in range(KD):
                        ins = nc.tensor.matmul(p_kv[:, g, :], KK[0:rows_in, t, g * P:(g + 1) * P],
                                               VX[0:rows_in, t, g, :], start=False, stop=final and g == KD - 1)
                    ins.then_inc(kv_mm.sem, 1)

                def body(c, s, n, last):
                    x_norm.wait(pe, c)
                    xt_ev.wait(pe, c - 1)
                    for k in range(KD):
                        for t in range(CH):
                            ins = nc.tensor.transpose(ps[k][:, t * P:(t + 1) * P], XN[s][:, t, k * P:(k + 1) * P],
                                                      ident[:, :])
                        ins.then_inc(x_tr.sem, 1)
                    xt_ev.wait(pe, c)
                    for t in range(CH):
                        pc, pt = (c, t - 2) if t >= 2 else (c - 1, t + 2)
                        h_ev.wait(pe, pc, pt + 1)
                        k_act.wait(pe, pc, pt + 1)
                        v_ev.wait(pe, pc, pt + 1)
                        for lo, hi, bank in ((C_H, C_K, 2), (C_K, C_END, 4)):
                            for k in range(KD):
                                ins = nc.tensor.matmul(ps[bank + t % 2][:, 0:hi - lo], XT[s][:, k, t * P:(t + 1) * P],
                                                       wcat[:, k, lo:hi], start=k == 0, stop=k == KD - 1)
                        ins.then_inc(hk_mm.sem, 1)
                        if t:
                            kv_sum(c, t - 1, last)
                    kv_sum(c, CH - 1, last)
                ring(pe, NCH, 2, body)
                pe.wait_ge(kv_mm.sem, CH * NCH)
                pe.sem_inc(kv_all, 1)

        r2 = Region(acc_t)
        r2.at = r2_from
        BX = [r2.take(CH, D) for _ in range(2)]
        BT = [r2.take(KD, CT) for _ in range(2)]
        QE, QR, QQ = r2.take(KD, CT), r2.take(KD, CT), r2.take(KD, CT)
        DR, MT = r2.take(KD, CT), r2.take(KD, CT)
        ML, MLT = r2.take(CH, D), r2.take(KD, CT)
        H1 = r2.take(2 * KD, CT)
        TM = r2.take(CH, D)
        bstats, bmv = r2.take(2, CH, 6), r2.take(2, CH, 2)
        brs, btv, btt = r2.take(2, CH), r2.take(2, CH), r2.take(2, CH)
        rw = Region(wf_t)
        s_strip = rw.take(W, HEADS)
        src_strip = rw.take(W, dt=i32)
        idx_blk = [rw.take(GB, dt=i32) for _ in range(2)]
        gat_blk = [rw.take(GB, HEADS) for _ in range(2)]
        rt = Region(work_t)
        neg_j = rt.take(STEPS)
        t_at = rt.at
        t_step = rt.take(STEPS, dt=i32, parts=1)
        j_step = work_t[32:33, t_at:t_at + STEPS].bitcast(i32)
        rt_from = rt.at
        kiota = rt.take(STEPS)
        cmp_f = [rt.take(512) for _ in range(2)]
        ones = rt.take(P)
        last_i, key = rt.take(KC, dt=i32), rt.take(KC)
        key_i, t_iota = rt.take(KC, dt=i32), rt.take(KC)

        base_in = [sem(f"base_in{s}") for s in range(2)]
        q_mm, q_act, q_dve = stage("q_mm", 2), stage("q_act", 2), stage("q_dve", 2)
        nd_mm, n_e, n_r, n_m = stage("nd_mm", 2), stage("n_e", 2), stage("n_r", 2), stage("n_m", 2)
        m_mm, m_st, m_ag, m_rs, m_norm = (stage("m_mm", CH), stage("m_st"), stage("m_ag"), stage("m_rs", 2 * RSQ),
                                          stage("m_norm"))
        m_tr, m_ev, u_mm, u_ev = stage("m_tr", 2), stage("m_ev", 2), stage("u_mm", 4), stage("u_ev", 4)
        o_mm, o_st, o_ag, o_norm, o_g, o_b, o_base = (stage("o_mm", CH), stage("o_st"), stage("o_ag"), stage("o_norm"),
                                                      stage("o_g"), stage("o_b"), stage("o_base"))
        st_b = [sem(f"st_b{s}") for s in range(2)]
        src_in, last_in = sem("src_in"), sem("last_in")
        idx_cp, gat_cp = stage("idx_cp"), stage("gat_cp")
        gat_in = [sem(f"gat_in{s}") for s in range(2)]
        io_set, key_set, cmp_set, cmp_mm, tab_set = sem("io_set"), sem("key_set"), sem("cmp_set"), sem("cmp_mm"), sem("tab_set")
        nseg = -(-STEPS // 512)

        with nc.Block() as block:
            @block.sync
            def _(sp):
                sp.dma_start(last_i, a["last_dst"]).then_inc(last_in, 16)
                sp.dma_start(BT[0], xnt_v[0]).then_inc(base_in[0], 16)
                sp.dma_start(BX[0], base_v[0]).then_inc(base_in[0], 16)

                def body(c, s, n, last):
                    if not last:
                        u_mm.wait(sp, c - 1)
                        pass_on(sp, "sp")
                        used(sp, st_b[1 - s], 16, n + s)
                        pass_on(sp, "sp")
                        sp.dma_start(BT[1 - s], at(xnt_v, c + 1)).then_inc(base_in[1 - s], 16)
                        sp.dma_start(BX[1 - s], at(base_v, c + 1)).then_inc(base_in[1 - s], 16)
                    o_base.wait(sp, c)
                    pass_on(sp, "sp")
                    sp.dma_start(at(base_v, c), BX[s]).then_inc(st_b[s], 16)
                ring(sp, NCH, 2, body)
                sp.wait_ge(st_b[0], 16 * ((NCH + 1) // 2))
                sp.wait_ge(st_b[1], 16 * (NCH // 2))

            @block.gpsimd
            def _(pool):
                nc.gpsimd.iota(kiota, pattern=[[1, STEPS]], base=0, channel_multiplier=0,
                               allow_small_or_imprecise_dtypes=True).then_inc(io_set, 1)
                nc.gpsimd.iota(t_iota, pattern=[[P, KC]], base=0, channel_multiplier=1,
                               allow_small_or_imprecise_dtypes=True).then_inc(io_set, 1)
                nc.gpsimd.memset(ones, 1.0).then_inc(io_set, 1)
                pool.dma_start(src_strip, a["src"].rearrange("(p w) -> p w", p=P)).then_inc(src_in, 16)
                pool.wait_ge(src_in, 16)
                nc.gpsimd.tensor_copy(idx_blk[0], src_strip[:, 0:GB]).then_inc(idx_cp.sem, 1)

                def blk(v, b, n):
                    return v[:, bass.ds(b * n, n)] if not isinstance(b, int) else v[:, b * n:(b + 1) * n]

                s_flat = s_strip.rearrange("p w h -> p (w h)")

                def body(b, s, n, last):
                    idx_cp.wait(pool, b)
                    gat_cp.wait(pool, b - 2)
                    pass_on(pool, "pool")
                    for q in range(GB):
                        pool.indirect_dma_start(gat_blk[s][:, q], None, as_tab,
                                                bass.IndirectOffsetOnAxis(idx_blk[s][:, q:q + 1], 0)
                                                ).then_inc(gat_in[s], 16)
                        if q == GB // 2 and not (isinstance(b, int) and b == 0):
                            pool.wait_ge(gat_in[1 - s], 16 * GB * (n + s))
                            nc.gpsimd.tensor_copy(blk(s_flat, b - 1, GB * HEADS),
                                                  gat_blk[1 - s].rearrange("p q h -> p (q h)")).then_inc(gat_cp.sem, 1)
                        if q == GB // 2 and not last:
                            nc.gpsimd.tensor_copy(idx_blk[1 - s], blk(src_strip, b + 1, GB)).then_inc(idx_cp.sem, 1)
                ring(pool, NBLK, 2, body)
                fin = (NBLK - 1) % 2
                pool.wait_ge(gat_in[fin], 16 * GB * ((NBLK - 1) // 2 + 1))
                nc.gpsimd.tensor_copy(s_flat[:, (NBLK - 1) * GB * HEADS:NBLK * GB * HEADS],
                                      gat_blk[fin].rearrange("p q h -> p (q h)")).then_inc(gat_cp.sem, 1)

            @block.vector
            def _(dve):
                dve.wait_ge(last_in, 16)
                dve.wait_ge(io_set, 3)
                nc.vector.tensor_scalar(key_i, last_i, 7, None, ALU.logical_shift_right).then_inc(key_set, 1)
                dve.wait_ge(key_set, 1)
                nc.vector.tensor_tensor(key, key_i, t_iota, ALU.add).then_inc(key_set, 1)
                dve.wait_ge(key_set, 2)
                for g in range(nseg):
                    w = min(512, STEPS - g * 512)
                    for k in range(KC):
                        i = g * KC + k
                        if i >= 2:
                            dve.wait_ge(cmp_mm, i - 1)
                        nc.vector.tensor_scalar(cmp_f[i % 2][:, 0:w], kiota[:, g * 512:g * 512 + w], key[:, k:k + 1],
                                                None, ALU.is_gt).then_inc(cmp_set, 1)
                    dve.wait_ge(cmp_mm, (g + 1) * KC)
                    seg = slice(g * 512, g * 512 + w)
                    nc.vector.tensor_copy(t_step[:, seg], ps[7][0:1, 0:w])
                    nc.vector.tensor_tensor(neg_j[:, seg], ps[7][:, 0:w], kiota[:, seg], ALU.subtract).then_inc(tab_set, 1)
                    dve.wait_ge(tab_set, 3 * g + 1)
                    nc.vector.tensor_scalar(j_step[:, seg], neg_j[32:33, seg], -1.0, None, ALU.mult).then_inc(tab_set, 1)
                    dve.wait_ge(tab_set, 3 * g + 2)
                    nc.vector.tensor_scalar(neg_j[:, seg], neg_j[:, seg], float(P), None, ALU.mult).then_inc(tab_set, 1)

                def body(c, s, n, last):
                    for m in range(2):
                        q_act.wait(dve, c, m + 1)
                        nd_mm.wait(dve, c - 1)
                        nc.vector.scalar_tensor_tensor(QQ[:, m], QE[:, m], 1.0, QR[:, m], ALU.min,
                                                       ALU.add).then_inc(q_dve.sem, 1)
                    for g in range(2):
                        n_e.wait(dve, c, g + 1)
                        nc.vector.reciprocal(DR[:, g], DR[:, g]).then_inc(n_r.sem, 1)
                        n_r.wait(dve, c, g + 1)
                        m_mm.wait(dve, c - 1)
                        nc.vector.tensor_tensor(MT[:, g], ps[2 + g][:, :], DR[:, g], ALU.mult).then_inc(n_m.sem, 1)
                    for t in range(CH):
                        m_mm.wait(dve, c, (t | 1) + 1)
                        ins = nc.vector.bn_stats(bstats[:, 0, t], ps[t // 2][:, (t % 2) * D:(t % 2 + 1) * D])
                    ins.then_inc(m_st.sem, 1)
                    m_st.wait(dve, c)
                    pass_on(dve, "dve")
                    for t in range(CH):
                        ins = nc.vector.bn_aggr(bmv[:, 0, t], bstats[:, 0, t])
                    ins.then_inc(m_ag.sem, 1)
                    m_ag.wait(dve, c)
                    rsqrt(dve, m_rs, c, 0, brs[:, 0], bmv[:, 0, :, 1], btv[:, 0], btt[:, 0], LN_EPS)
                    for t in range(CH):
                        ins = nc.vector.tensor_scalar(ML[:, t], ps[t // 2][:, (t % 2) * D:(t % 2 + 1) * D],
                                                      bmv[:, 0, t, 0:1], brs[:, 0, t:t + 1], ALU.subtract, ALU.mult)
                    ins.then_inc(m_norm.sem, 1)
                    for t in range(CH):
                        o_mm.wait(dve, c, (t | 1) + 1)
                        ins = nc.vector.bn_stats(bstats[:, 1, t], ps[4 + t // 2][:, (t % 2) * D:(t % 2 + 1) * D])
                    ins.then_inc(o_st.sem, 1)
                    o_st.wait(dve, c)
                    pass_on(dve, "dve")
                    for t in range(CH):
                        ins = nc.vector.bn_aggr(bmv[:, 1, t], bstats[:, 1, t])
                    ins.then_inc(o_ag.sem, 1)
                    o_ag.wait(dve, c)
                    rsqrt(dve, m_rs, c, RSQ, brs[:, 1], bmv[:, 1, :, 1], btv[:, 1], btt[:, 1], LN_EPS)
                    for t in range(CH):
                        ins = nc.vector.tensor_scalar(TM[:, t], ps[4 + t // 2][:, (t % 2) * D:(t % 2 + 1) * D],
                                                      bmv[:, 1, t, 0:1], brs[:, 1, t:t + 1], ALU.subtract, ALU.mult)
                    ins.then_inc(o_norm.sem, 1)
                    o_norm.wait(dve, c)
                    nc.vector.tensor_tensor(TM, TM, row(R_G2).unsqueeze(1).broadcast_to([P, CH, D]),
                                            ALU.mult).then_inc(o_g.sem, 1)
                    o_g.wait(dve, c)
                    nc.vector.tensor_tensor(TM, TM, row(R_B2).unsqueeze(1).broadcast_to([P, CH, D]),
                                            ALU.add).then_inc(o_b.sem, 1)
                    o_b.wait(dve, c)
                    dve.wait_ge(base_in[s], 32 * (n + 1))
                    nc.vector.tensor_tensor(BX[s], BX[s], TM, ALU.add).then_inc(o_base.sem, 1)
                ring(dve, NCH, 2, body)

            @block.scalar
            def _(act):

                def body(c, s, n, last):
                    for m in range(2):
                        q_mm.wait(act, c, m + 1)
                        q_dve.wait(act, c - 1, m + 1)
                        nc.scalar.activation(QE[:, m], ps[m][:, :], ACT.Exp)
                        nc.scalar.activation(QR[:, m], ps[m][:, :], ACT.Relu).then_inc(q_act.sem, 1)
                    for g in range(2):
                        nd_mm.wait(act, c, g + 1)
                        n_m.wait(act, c - 1, g + 1)
                        nc.scalar.activation(DR[:, g], ps[4 + g][:, :], ACT.Copy, bias=ATT_EPS).then_inc(n_e.sem, 1)
                    for k in range(KD):
                        m_tr.wait(act, c, k + 1)
                        u_mm.wait(act, c - 1)
                        nc.scalar.activation(MLT[:, k], ps[2 + k][:, :], ACT.Identity, scale=cols[:, Q_MG + k:Q_MG + k + 1],
                                             bias=cols[:, Q_MB + k:Q_MB + k + 1]).then_inc(m_ev.sem, 1)
                    for m in range(4):
                        u_mm.wait(act, c, m + 1)
                        o_mm.wait(act, c - 1)
                        nc.scalar.activation(H1[:, m], ps[(0, 1, 6, 3)[m]][:, :], ACT.Relu).then_inc(u_ev.sem, 1)
                ring(act, NCH, 2, body)

            @block.tensor
            def _(pe):
                for g in range(nseg):
                    w = min(512, STEPS - g * 512)
                    if g:
                        pe.wait_ge(tab_set, 3 * g)
                    for k in range(KC):
                        i = g * KC + k
                        pe.wait_ge(cmp_set, i + 1)
                        nc.tensor.matmul(ps[7][:, 0:w], ones, cmp_f[i % 2][:, 0:w], start=k == 0,
                                         stop=k == KC - 1).then_inc(cmp_mm, 1)

                def body(c, s, n, last):
                    pe.wait_ge(base_in[s], 32 * (n + 1))
                    u_ev.wait(pe, c - 1)
                    for m in range(2):
                        for k in range(KD):
                            ins = nc.tensor.matmul(ps[m][:, :], wq[:, k, m * P:(m + 1) * P], BT[s][:, k, :],
                                                   start=k == 0, stop=k == KD - 1)
                        ins.then_inc(q_mm.sem, 1)
                    o_norm.wait(pe, c - 1)
                    for g in range(2):
                        q_dve.wait(pe, c, g + 1)
                        nc.tensor.matmul(ps[2 + g][:, :], kvbd[:, g], QQ[:, g], start=True, stop=True)
                        nc.tensor.matmul(ps[4 + g][:, :], ksbd[:, g], QQ[:, g], start=True, stop=True).then_inc(nd_mm.sem, 1)
                    n_m.wait(pe, c)
                    for t in range(CH):
                        for k in range(KD):
                            ins = nc.tensor.matmul(ps[t // 2][:, (t % 2) * D:(t % 2 + 1) * D], MT[:, k, t * P:(t + 1) * P],
                                                   wm[:, k, :], start=k == 0, stop=k == KD - 1)
                        ins.then_inc(m_mm.sem, 1)
                    m_norm.wait(pe, c)
                    for k in range(KD):
                        for t in range(CH):
                            ins = nc.tensor.transpose(ps[2 + k][:, t * P:(t + 1) * P], ML[:, t, k * P:(k + 1) * P],
                                                      ident[:, :])
                        ins.then_inc(m_tr.sem, 1)
                    m_ev.wait(pe, c)
                    for m in range(4):
                        for k in range(4):
                            rhs = BT[s][:, k, :] if k < 2 else MLT[:, k - 2, :]
                            ins = nc.tensor.matmul(ps[(0, 1, 6, 3)[m]][:, :], w1[:, k, m * P:(m + 1) * P], rhs,
                                                   start=k == 0, stop=k == 3)
                        ins.then_inc(u_mm.sem, 1)
                    u_ev.wait(pe, c)
                    for t in range(CH):
                        for k in range(4):
                            ins = nc.tensor.matmul(ps[4 + t // 2][:, (t % 2) * D:(t % 2 + 1) * D],
                                                   H1[:, k, t * P:(t + 1) * P], w2[:, k, :], start=k == 0, stop=k == 3)
                        ins.then_inc(o_mm.sem, 1)
                ring(pe, NCH, 2, body)

        r3 = Region(acc_t)
        rec = r3.take(W, RECW)
        gap_prev, gap_next = r3.take(W), r3.take(W)
        run = r3.take(W)
        rw3 = Region(wf_t)
        rw3.at = rw.at
        dst_i, oth_i = r3.take(W, dt=i32), rw3.take(W, dt=i32)
        edge_end = r3.take(3, HEADS)
        lt = r3.take(3, P, parts=HEADS)
        carry = r3.take(HEADS, P + 1, parts=HEADS)
        padrow = r3.take(RECW)
        s3_in, s3_gap, s3_scan, s3_tr, s3_lt, s3_car, s3_ctr, s3_cc, s3_rec, s3_st, s3_pad = (
            sem("s3_in"), sem("s3_gap"), sem("s3_scan"), sem("s3_tr"), sem("s3_lt"), sem("s3_car"), sem("s3_ctr"),
            sem("s3_cc"), sem("s3_rec"), sem("s3_st"), sem("s3_pad"))
        s3_end = sem("s3_end")
        strip = lambda name: a[name].rearrange("(p w) -> p w", p=P)

        with nc.Block() as block:
            @block.sync
            def _(sp):
                sp.dma_start(dst_i, strip("dst")).then_inc(s3_in, 16)
                sp.dma_start(oth_i, strip("dst_prev")).then_inc(s3_in, 16)
                sp.wait_ge(s3_gap, 1)
                sp.dma_start(oth_i, strip("dst_next")).then_inc(s3_in, 16)
                sp.wait_ge(s3_pad, 3)
                sp.dma_start(rec_tab[TE * P:(TE + 1) * P, :], padrow).then_inc(s3_st, 16)
                sp.wait_ge(s3_rec, 1)
                sp.dma_start(rec_tab[0:EP, :].rearrange("(p w) r -> p w r", p=P), rec).then_inc(s3_st, 16)
                sp.wait_ge(s3_st, 32)

            @block.scalar
            def _(act):
                act.wait_ge(s3_in, 48)
                nc.scalar.activation(rec[:, :, 1], dst_i, ACT.Copy)
                nc.scalar.activation(rec[:, :, 2:6], s_strip, ACT.Copy).then_inc(s3_cc, 1)

            @block.gpsimd
            def _(pool):
                nc.gpsimd.tensor_copy(rec[:, :, 0:1].bitcast(i32).rearrange("p w o -> p (w o)"), src_strip)
                nc.gpsimd.memset(padrow, 0.0).then_inc(s3_pad, 1)
                pool.wait_ge(s3_pad, 1)
                nc.gpsimd.memset(padrow[:, 1:2], -1.0).then_inc(s3_pad, 2)

            @block.vector
            def _(dve):
                v = [0]

                def link(ins):
                    v[0] += 1
                    ins.then_inc(s3_scan, 1)
                    dve.wait_ge(s3_scan, v[0])

                dve.wait_ge(s3_in, 32)
                nc.vector.tensor_tensor(gap_prev, dst_i, oth_i, ALU.not_equal).then_inc(s3_gap, 1)
                dve.wait_ge(s3_gap, 1)
                link(nc.vector.tensor_scalar(gap_prev, gap_prev, -BIG, None, ALU.mult))
                dve.wait_ge(s3_in, 48)
                link(nc.vector.tensor_tensor(gap_next, dst_i, oth_i, ALU.not_equal))
                link(nc.vector.tensor_scalar(gap_next, gap_next, -BIG, None, ALU.mult))

                def carried(d, gap):
                    nc.vector.tensor_reduce(edge_end[:, 1], gap.unsqueeze(1).broadcast_to([P, HEADS, W]), AX.X,
                                            ALU.min).then_inc(s3_end, 1)
                    dve.wait_ge(s3_tr, 2 * d + 1)
                    link(nc.vector.tensor_copy(lt[:, 0:2], ps[0][0:HEADS, 0:2 * P].rearrange("p (a b) -> p a b", a=2)))
                    cr = carry[:, d]
                    link(nc.vector.memset(cr, -BIG))
                    if d == 0:
                        link(nc.vector.tensor_tensor_scan(cr[:, 1:P + 1], lt[:, 1], lt[:, 0], -BIG, ALU.add, ALU.max))
                    else:
                        link(nc.vector.tensor_tensor_scan(cr[:, 0:P][:, ::-1], lt[:, 1][:, ::-1], lt[:, 0][:, ::-1],
                                                          -BIG, ALU.add, ALU.max))
                    dve.sem_inc(s3_car, 1)
                    dve.wait_ge(s3_tr, 2 * d + 2)
                    link(nc.vector.tensor_copy(edge_end[:, 2], ps[1][:, 0:HEADS]))

                for h in range(HEADS):
                    link(nc.vector.tensor_tensor_scan(run, gap_prev, s_strip[:, :, h], -BIG, ALU.add, ALU.max))
                    link(nc.vector.tensor_copy(edge_end[:, 0, h:h + 1], run[:, W - 1:W]))
                carried(0, gap_prev)
                for h in range(HEADS):
                    link(nc.vector.tensor_tensor_scan(rec[:, :, 6 + h], gap_prev, s_strip[:, :, h],
                                                      edge_end[:, 2, h:h + 1], ALU.add, ALU.max))
                for h in range(HEADS):
                    link(nc.vector.tensor_tensor_scan(run[:, ::-1], gap_next[:, ::-1], rec[:, :, 6 + h][:, ::-1],
                                                      -BIG, ALU.add, ALU.max))
                    link(nc.vector.tensor_copy(edge_end[:, 0, h:h + 1], run[:, 0:1]))
                carried(1, gap_next)
                for h in range(HEADS):
                    link(nc.vector.tensor_tensor_scan(run[:, ::-1], gap_next[:, ::-1], rec[:, :, 6 + h][:, ::-1],
                                                      edge_end[:, 2, h:h + 1], ALU.add, ALU.max))
                    link(nc.vector.tensor_copy(rec[:, :, 6 + h], run))
                dve.wait_ge(s3_cc, 1)
                dve.wait_ge(s3_pad, 3)
                dve.sem_inc(s3_rec, 1)

            @block.tensor
            def _(pe):
                for d in range(2):
                    pe.wait_ge(s3_end, d + 1)
                    for j in range(2):
                        ins = nc.tensor.transpose(ps[0][0:HEADS, j * P:(j + 1) * P], edge_end[:, j], ident[:, :])
                    ins.then_inc(s3_tr, 1)
                    pe.wait_ge(s3_car, d + 1)
                    src = carry[:, 0, 0:P] if d == 0 else carry[:, 1, 1:P + 1]
                    nc.tensor.transpose(ps[1][:, 0:HEADS], src, ident[0:HEADS, 0:HEADS]).then_inc(s3_tr, 1)

        r4 = Region(work_t)
        r4.at = rt_from
        RECS = [r4.take(GU, RECW) for _ in range(4)]
        ad_all = r4.take(NT, HEADS)
        G = [r4.take(GU, MW) for _ in range(4)]
        S = [r4.take(GU, P) for _ in range(4)]
        ST = r4.take(GU, P)
        dr = r4.take(GU)
        zz, lk = r4.take(GU, 2, HEADS), r4.take(GU, 2, HEADS)
        df = r4.take(GU, HEADS)
        bnt = [r4.take(16) for _ in range(3)]
        W1F, W2F, WOF = (wf_t[:, i * NEXP * KD * D:(i + 1) * NEXP * KD * D].rearrange("p (e n) -> p e n", n=D)
                         for i in range(3))
        rec_in = [sem(f"rec_in{s}") for s in range(4)]
        ad_in = sem("ad_in")
        g_in = [sem(f"g_in{s}") for s in range(4)]
        dr_set, s_set, t_mm, st_ev, d_mm = stage("dr_set"), stage("s_set", GU), stage("t_mm"), stage("st_ev"), stage("d_mm")
        z_set, l_set, p_df, p_exp, msg_set = stage("z_set"), stage("l_set"), stage("p_df"), stage("p_exp"), stage("msg_set")
        g_mm, acc_add = stage("g_mm", GU), stage("acc_add", GU)
        acc_zero, wf_in, bn_st = sem("acc_zero"), sem("wf_in"), stage("bn_st", 2 * (RSQ + 2))
        rec_v = rec_tab.rearrange("(t p) r -> t p r", p=P)

        def more(b, by):
            return not (isinstance(b, int) and b + by >= NB)

        BOUND = "the tables hold edge tiles up to TE and node tiles below NT by their making"

        def step_values(engine, table, b, most):
            lo = b * GU
            sl = table[:, lo:lo + GU] if isinstance(b, int) else table[:, bass.ds(lo, GU)]
            return nc.values_load_multi_w_load_instructions(sl, engines=[engine], min_val=0, max_val=most,
                                                            skip_runtime_bounds_check_because=BOUND)[1]

        with nc.Block() as block:
            @block.sync
            def _(sp):
                def body(b, s, n, last):
                    ts = step_values(ET.SP, t_step, b, TE)
                    msg_set.wait(sp, b - 4)
                    pass_on(sp, "sp")
                    for u in range(GU):
                        sp.dma_start(RECS[s][:, u], rec_v[bass.ds(ts[u], 1)].rearrange("o p r -> (o p) r")
                                     ).then_inc(rec_in[s], 16)
                sp.dma_start(ad_all, ad_tab.rearrange("(t p) r -> p t r", p=P)).then_inc(ad_in, 16)
                ring(sp, NB, 4, body)
                sp.wait_ge(wf_in, 48)

            @block.gpsimd
            def _(pool):
                def body(b, s, n, last):
                    pool.wait_ge(rec_in[s], 64 * (n + 1))
                    g_mm.wait(pool, b - 4)
                    pass_on(pool, "pool")
                    for u in range(GU):
                        pool.indirect_dma_start(G[s][:, u, 0:D], None, h_tab,
                                                bass.IndirectOffsetOnAxis(RECS[s][:, u, 0:1].bitcast(i32), 0)
                                                ).then_inc(g_in[s], 16)
                ring(pool, NB, 4, body)

            @block.vector
            def _(dve):
                def relative(b, s, n):
                    dve.wait_ge(rec_in[s], 64 * (n + 1))
                    s_set.wait(dve, b - 1)
                    nj = neg_j[:, b * GU:(b + 1) * GU] if isinstance(b, int) else neg_j[:, bass.ds(b * GU, GU)]
                    nc.vector.tensor_tensor(dr, RECS[s][:, :, 1], nj, ALU.add).then_inc(dr_set.sem, 1)

                def onehot(b, s, u):
                    dr_set.wait(dve, b)
                    nc.vector.tensor_scalar(S[s][:, u], iota_row[:, :], dr[:, u:u + 1], None, ALU.is_equal
                                            ).then_inc(s_set.sem, 1)

                def logits(b, s):
                    d_mm.wait(dve, b)
                    d_e = ps[5][:, 0:GU * HEADS].rearrange("p (u h) -> p u h", u=GU)
                    nc.vector.tensor_tensor(zz, RECS[s][:, :, 2:10].rearrange("p u (a h) -> p u a h", a=2),
                                            d_e.unsqueeze(2).broadcast_to([P, GU, 2, HEADS]), ALU.add
                                            ).then_inc(z_set.sem, 1)

                def leaky(b):
                    z_set.wait(dve, b)
                    zf, lf = zz.rearrange("p u a h -> p (u a h)"), lk.rearrange("p u a h -> p (u a h)")
                    nc.vector.scalar_tensor_tensor(lf, zf, 0.2, zf, ALU.mult, ALU.max).then_inc(l_set.sem, 1)

                def difference(b):
                    l_set.wait(dve, b)
                    nc.vector.tensor_tensor(df, lk[:, :, 0], lk[:, :, 1], ALU.subtract).then_inc(p_df.sem, 1)

                def message(b, s, n):
                    p_exp.wait(dve, b)
                    dve.wait_ge(g_in[s], 64 * (n + 1))
                    msg = G[s][:, :, 0:D].rearrange("p u (h c) -> p u h c", h=HEADS)
                    nc.vector.tensor_tensor(msg, msg, G[s][:, :, D:MW].unsqueeze(3).broadcast_to([P, GU, HEADS, D // HEADS]),
                                            ALU.mult).then_inc(msg_set.sem, 1)

                def add(b, u, j):
                    g_mm.wait(dve, b, u + 1)
                    if u:
                        acc_add.wait(dve, b, u)
                    else:
                        acc_add.wait(dve, b - 1)
                        if isinstance(b, int) and b == 0:
                            dve.wait_ge(acc_zero, 2)
                    aj = acc[:, bass.ds(j, 1)].rearrange("p o c -> p (o c)")
                    nc.vector.tensor_tensor(aj, aj, ps[u][:, 0:MW], ALU.add).then_inc(acc_add.sem, 1)

                for b in range(3):
                    relative(b, b, 0)
                    for u in range(GU):
                        onehot(b, b, u)
                for b in range(2):
                    logits(b, b)
                    leaky(b)
                    difference(b)
                    if b == 0:
                        message(0, 0, 0)
                half = NT * MW // 2
                nc.vector.memset(acc_t[:, 0:half], 0.0).then_inc(acc_zero, 1)
                k = 0
                for j, (qb, qg, qbe, qm, qv) in enumerate(((Q_B1, Q_G1, Q_BE1, Q_M1, Q_V1), (Q_B2, Q_G2, Q_BE2, Q_M2, Q_V2))):
                    sc, of = bn[:, 32 * j:32 * j + 16], bn[:, 32 * j + 16:32 * j + 32]
                    col = lambda q: cols[:, q:q + 16]
                    k = rsqrt(dve, bn_st, 0, k, sc, col(qv), bnt[0], bnt[1], BN_EPS)
                    nc.vector.tensor_tensor(sc, sc, col(qg), ALU.mult)
                    nc.vector.tensor_tensor(bnt[2], col(qb), col(qm), ALU.subtract).then_inc(bn_st.sem, 1)
                    bn_st.wait(dve, 0, k + 1)
                    nc.vector.tensor_tensor(bnt[2], bnt[2], sc, ALU.mult).then_inc(bn_st.sem, 1)
                    bn_st.wait(dve, 0, k + 2)
                    k += 2
                    nc.vector.tensor_tensor(of, bnt[2], col(qbe), ALU.add)

                def body(b, s, n, last):
                    s2, s3, n3 = (s + 2) % 4, (s + 3) % 4, n + (s >= 1)
                    if more(b, 1):
                        message(b + 1, (s + 1) % 4, n + (s >= 3))
                    js = step_values(ET.DVE, j_step, b, NT - 1)
                    add(b, 0, js[0])
                    if more(b, 3):
                        relative(b + 3, s3, n3)
                        onehot(b + 3, s3, 0)
                        onehot(b + 3, s3, 1)
                    add(b, 1, js[1])
                    if more(b, 2):
                        logits(b + 2, s2)
                    if more(b, 3):
                        onehot(b + 3, s3, 2)
                    if more(b, 2):
                        leaky(b + 2)
                    add(b, 2, js[2])
                    if more(b, 3):
                        onehot(b + 3, s3, 3)
                    if more(b, 2):
                        difference(b + 2)
                    add(b, 3, js[3])
                ring(dve, NB, 4, body, ahead=3)

            @block.scalar
            def _(act):
                for w, name in ((W1F, "L0_ffn_W1"), (W2F, "L0_ffn_W2"), (WOF, "L0_ffn_Wo")):
                    act.dma_start(w, a[name].rearrange("e (k p) n -> p (e k) n", p=P)).then_inc(wf_in, 16)
                half = NT * MW // 2
                nc.scalar.memzero(acc_t[:, half:NT * MW]).then_inc(acc_zero, 1)

                def transposed(b):
                    t_mm.wait(act, b)
                    d_mm.wait(act, b - 1)
                    nc.scalar.activation(ST.rearrange("p u n -> p (u n)"), ps[4][:, :], ACT.Copy).then_inc(st_ev.sem, 1)

                def exponent(b, s):
                    p_df.wait(act, b)
                    g_mm.wait(act, b - 4)
                    nc.scalar.activation(G[s][:, :, D:MW], df, ACT.Exp).then_inc(p_exp.sem, 1)
                for b in range(2):
                    transposed(b)
                    exponent(b, b)

                def body(b, s, n, last):
                    if more(b, 2):
                        transposed(b + 2)
                        exponent(b + 2, (s + 2) % 4)
                ring(act, NB, 4, body, ahead=3)

            @block.tensor
            def _(pe):
                def transpose(b, s):
                    s_set.wait(pe, b)
                    st_ev.wait(pe, b - 1)
                    for u in range(GU):
                        ins = nc.tensor.transpose(ps[4][:, u * P:(u + 1) * P], S[s][:, u], ident[:, :])
                    ins.then_inc(t_mm.sem, 1)

                def dst_logits(b, js):
                    st_ev.wait(pe, b)
                    z_set.wait(pe, b - 1)
                    for u in range(GU):
                        ins = nc.tensor.matmul(ps[5][:, u * HEADS:(u + 1) * HEADS], ST[:, u],
                                               ad_all[:, bass.ds(js[u], 1)].rearrange("p o h -> p (o h)"),
                                               start=True, stop=True)
                    ins.then_inc(d_mm.sem, 1)
                pe.wait_ge(ad_in, 16)
                for b in range(2):
                    transpose(b, b)
                    dst_logits(b, step_values(ET.PE, j_step, b, NT - 1))

                def body(b, s, n, last):
                    if more(b, 2):
                        js = step_values(ET.PE, j_step, b + 2, NT - 1)
                    msg_set.wait(pe, b)
                    for u in range(GU):
                        acc_add.wait(pe, b - 1, u + 1)
                        nc.tensor.matmul(ps[u][:, 0:MW], S[s][:, u], G[s][:, u], start=True,
                                         stop=True).then_inc(g_mm.sem, 1)
                        if u == 0 and more(b, 2):
                            transpose(b + 2, (s + 2) % 4)
                        if u == 1 and more(b, 2):
                            dst_logits(b + 2, js)
                ring(pe, NB, 4, body, ahead=3)

        r5 = Region(work_t)
        Y = [r5.take(CH, D) for _ in range(2)]
        O, XF = r5.take(CH, D), r5.take(CH, D)
        XFT = [r5.take(KD, CT) for _ in range(2)]
        HA = [r5.take(KD, CT) for _ in range(2)]
        HB = [r5.take(KD, CT) for _ in range(2)]
        rden = r5.take(CH, HEADS)
        lg, ex = r5.take(CH, NEXP), r5.take(CH, NEXP)
        WT8 = [r5.take(CH, NEXP) for _ in range(2)]
        mx, sm = r5.take(CH), r5.take(CH)
        wT = r5.take(CT, parts=NEXP)
        cst, cmv = r5.take(2, CH, 6), r5.take(2, CH, 2)
        crs, ctv, ctt = r5.take(2, CH), r5.take(2, CH), r5.take(2, CH)
        y_in = [sem(f"y_in{s}") for s in range(2)]
        st_o = [sem(f"st_o{s}") for s in range(2)]
        prep = stage("prep", 14)
        c_rs, xf_tr, xf_ev, lg_mm, ex_act = stage("c_rs", 2 * RSQ), stage("xf_tr", 2), stage("xf_ev", 2), stage("lg_mm"), stage("ex_act")
        xf_norm, lg_sub, w_set, w_tr, w_ev, bo_mm, y_init = (stage("xf_norm"), stage("lg_sub"), stage("w_set"),
                                                             stage("w_tr"), stage("w_ev"), stage("bo_mm"), stage("y_init"))
        lg_st = stage("lg_st", 4)
        a_mm, a_ev, b_mm, b_ev = (stage(x, 2 * NEXP) for x in ("a_mm", "a_ev", "b_mm", "b_ev"))
        o2_mm, y_acc = stage("o2_mm", NEXP * 2), stage("y_acc", NEXP)

        with nc.Block() as block:
            @block.sync
            def _(sp):
                sp.dma_start(Y[0], base_v[0]).then_inc(y_in[0], 16)

                def body(c, s, n, last):
                    if not last:
                        used(sp, st_o[1 - s], 16, n + s)
                        pass_on(sp, "sp")
                        sp.dma_start(Y[1 - s], at(base_v, c + 1)).then_inc(y_in[1 - s], 16)
                    y_acc.wait(sp, c)
                    pass_on(sp, "sp")
                    sp.dma_start(at(out_v, c), Y[s]).then_inc(st_o[s], 16)
                ring(sp, NCH, 2, body)
                sp.wait_ge(st_o[0], 16 * ((NCH + 1) // 2))
                sp.wait_ge(st_o[1], 16 * (NCH // 2))

            @block.vector
            def _(dve):
                def wide(at_):
                    return row(at_).unsqueeze(1).broadcast_to([P, CH, D])

                def link(c, k, ins):
                    ins.then_inc(prep.sem, 1)
                    prep.wait(dve, c, k)

                def gat_sums(c):
                    aj = acc[:, c * CH:(c + 1) * CH] if isinstance(c, int) else acc[:, bass.ds(c * CH, CH)]
                    link(c, 1, nc.vector.tensor_scalar(rden, aj[:, :, D:MW], 1e-16, None, ALU.max))
                    link(c, 2, nc.vector.reciprocal(rden, rden))
                    for t in range(CH):
                        ins = nc.vector.tensor_tensor(O[:, t].rearrange("p (h c) -> p h c", h=HEADS),
                                                      aj[:, t, 0:D].rearrange("p (h c) -> p h c", h=HEADS),
                                                      rden[:, t].unsqueeze(2).broadcast_to([P, HEADS, D // HEADS]), ALU.mult)
                    link(c, 3, ins)
                    link(c, 4, nc.vector.tensor_tensor(O, O, wide(R_BIAS), ALU.add))
                    for t in range(CH):
                        ins = nc.vector.bn_stats(cst[:, 0, t], O[:, t])
                    link(c, 5, ins)
                    pass_on(dve, "dve")
                    for t in range(CH):
                        ins = nc.vector.bn_aggr(cmv[:, 0, t], cst[:, 0, t])
                    link(c, 6, ins)

                def gat_norm(c):
                    rsqrt(dve, c_rs, c, 0, crs[:, 0], cmv[:, 0, :, 1], ctv[:, 0], ctt[:, 0], LN_EPS)
                    for t in range(CH):
                        ins = nc.vector.tensor_scalar(O[:, t], O[:, t], cmv[:, 0, t, 0:1], crs[:, 0, t:t + 1],
                                                      ALU.subtract, ALU.mult)
                    link(c, 7, ins)
                    link(c, 8, nc.vector.tensor_tensor(O, O, wide(R_GAMMA), ALU.mult))
                    link(c, 9, nc.vector.tensor_tensor(O, O, wide(R_BETA), ALU.add))

                def branches(c, s, n):
                    dve.wait_ge(y_in[s], 16 * (n + 1))
                    xf_tr.wait(dve, c - 1)
                    for t in range(CH):
                        ins = nc.vector.scalar_tensor_tensor(XF[:, t], O[:, t], 0.0, row(R_PRELU), ALU.min, ALU.mult)
                    link(c, 10, ins)
                    of, yf, xf = (v.rearrange("p t d -> p (t d)") for v in (O, Y[s], XF))
                    link(c, 11, nc.vector.scalar_tensor_tensor(yf, of, 0.0, yf, ALU.max, ALU.add))
                    link(c, 12, nc.vector.tensor_tensor(yf, yf, xf, ALU.add))

                def second_norm(c, s):
                    for t in range(CH):
                        ins = nc.vector.bn_stats(cst[:, 1, t], Y[s][:, t])
                    link(c, 13, ins)
                    pass_on(dve, "dve")
                    for t in range(CH):
                        ins = nc.vector.bn_aggr(cmv[:, 1, t], cst[:, 1, t])
                    link(c, 14, ins)
                    rsqrt(dve, c_rs, c, RSQ, crs[:, 1], cmv[:, 1, :, 1], ctv[:, 1], ctt[:, 1], LN_EPS)

                def second_apply(c, s):
                    for t in range(CH):
                        ins = nc.vector.tensor_scalar(XF[:, t], Y[s][:, t], cmv[:, 1, t, 0:1], crs[:, 1, t:t + 1],
                                                      ALU.subtract, ALU.mult)
                    ins.then_inc(xf_norm.sem, 1)

                def router_logits(c):
                    lg_mm.wait(dve, c)
                    br = rows[:, R_BR:R_BR + NEXP].unsqueeze(1).broadcast_to([P, CH, NEXP])
                    nc.vector.tensor_tensor(lg, ps[7][:, 0:CH * NEXP].rearrange("p (t e) -> p t e", t=CH), br,
                                            ALU.add).then_inc(lg_st.sem, 1)
                    lg_st.wait(dve, c, 1)
                    nc.vector.tensor_reduce(mx, lg, AX.X, ALU.max).then_inc(lg_st.sem, 1)
                    lg_st.wait(dve, c, 2)
                    nc.vector.tensor_tensor(lg, lg, mx.unsqueeze(2).broadcast_to([P, CH, NEXP]),
                                            ALU.subtract).then_inc(lg_sub.sem, 1)

                def router_weights(c, s):
                    ex_act.wait(dve, c)
                    nc.vector.tensor_reduce(sm, ex, AX.X, ALU.add).then_inc(lg_st.sem, 1)
                    lg_st.wait(dve, c, 3)
                    nc.vector.reciprocal(sm, sm).then_inc(lg_st.sem, 1)
                    lg_st.wait(dve, c, 4)
                    nc.vector.tensor_tensor(WT8[s], ex, sm.unsqueeze(2).broadcast_to([P, CH, NEXP]),
                                            ALU.mult).then_inc(w_set.sem, 1)

                def expert(c, s, e):
                    for t in range(CH):
                        if t % 2 == 0:
                            o2_mm.wait(dve, c, 2 * e + t // 2 + 1)
                            if e:
                                y_acc.wait(dve, c, e)
                        ins = nc.vector.scalar_tensor_tensor(Y[s][:, t], ps[4 + t // 2][:, (t % 2) * D:(t % 2 + 1) * D],
                                                             WT8[s][:, t, e:e + 1], Y[s][:, t], ALU.mult, ALU.add)
                    ins.then_inc(y_acc.sem, 1)

                gat_sums(0)
                gat_norm(0)
                branches(0, 0, 0)
                second_norm(0, 0)
                second_apply(0, 0)
                router_logits(0)
                router_weights(0, 0)

                def body(c, s, n, last):
                    bo_mm.wait(dve, c)
                    for j in range(2):
                        yj = Y[s][:, 2 * j:2 * j + 2].rearrange("p t d -> p (t d)")
                        ins = nc.vector.tensor_tensor(yj, yj, ps[6 + j][:, :], ALU.add)
                    ins.then_inc(y_init.sem, 1)
                    y_init.wait(dve, c)
                    for e in range(NEXP):
                        expert(c, s, e)
                        if last:
                            continue
                        if e == 0:
                            gat_sums(c + 1)
                        if e == 1:
                            gat_norm(c + 1)
                        if e == 2:
                            branches(c + 1, 1 - s, n + s)
                        if e == 3:
                            second_norm(c + 1, 1 - s)
                        if e == 4:
                            second_apply(c + 1, 1 - s)
                        if e == 6:
                            router_logits(c + 1)
                        if e == 7:
                            router_weights(c + 1, 1 - s)
                ring(dve, NCH, 2, body)

            @block.scalar
            def _(act):
                def layer_1(c, e):
                    for m in range(KD):
                        a_mm.wait(act, c, 2 * e + m + 1)
                        i = 2 * e + m
                        nc.scalar.activation(HA[e % 2][:, m], ps[m][:, :], ACT.Relu, scale=bn[:, i:i + 1],
                                             bias=bn[:, 16 + i:17 + i]).then_inc(a_ev.sem, 1)

                def layer_2(c, e):
                    for m in range(KD):
                        b_mm.wait(act, c, 2 * e + m + 1)
                        i = 2 * e + m
                        nc.scalar.activation(HB[e % 2][:, m], ps[2 + m][:, :], ACT.Relu, scale=bn[:, 32 + i:33 + i],
                                             bias=bn[:, 48 + i:49 + i]).then_inc(b_ev.sem, 1)

                def xf_out(c, s):
                    for k in range(KD):
                        xf_tr.wait(act, c, k + 1)
                        nc.scalar.activation(XFT[s][:, k], ps[6 + k][:, :], ACT.Copy).then_inc(xf_ev.sem, 1)

                def router_exp(c):
                    lg_sub.wait(act, c)
                    nc.scalar.activation(ex, lg, ACT.Exp).then_inc(ex_act.sem, 1)

                xf_out(0, 0)
                router_exp(0)
                layer_1(0, 0)

                def body(c, s, n, last):
                    for e in range(NEXP):
                        if e < NEXP - 1:
                            layer_1(c, e + 1)
                        elif not last:
                            layer_1(c + 1, 0)
                        if e == 0:
                            w_tr.wait(act, c)
                            nc.scalar.activation(wT, ps[6][0:NEXP, :], ACT.Copy).then_inc(w_ev.sem, 1)
                        layer_2(c, e)
                        if e == 5 and not last:
                            xf_out(c + 1, 1 - s)
                        if e == 7 and not last:
                            router_exp(c + 1)
                ring(act, NCH, 2, body)

            @block.tensor
            def _(pe):
                def layer_1(c, s, e):
                    if e == 0:
                        xf_ev.wait(pe, c)
                        a_ev.wait(pe, c - 1)
                    else:
                        a_ev.wait(pe, c, 2 * e)
                    for m in range(KD):
                        for k in range(KD):
                            ins = nc.tensor.matmul(ps[m][:, :], W1F[:, 2 * e + k, m * P:(m + 1) * P], XFT[s][:, k],
                                                   start=k == 0, stop=k == KD - 1)
                        ins.then_inc(a_mm.sem, 1)

                def layer_2(c, e):
                    a_ev.wait(pe, c, 2 * e + 2)
                    if e:
                        b_ev.wait(pe, c, 2 * e)
                    else:
                        b_ev.wait(pe, c - 1)
                    for m in range(KD):
                        for k in range(KD):
                            ins = nc.tensor.matmul(ps[2 + m][:, :], W2F[:, 2 * e + k, m * P:(m + 1) * P], HA[e % 2][:, k],
                                                   start=k == 0, stop=k == KD - 1)
                        ins.then_inc(b_mm.sem, 1)

                def layer_3(c, e):
                    b_ev.wait(pe, c, 2 * e + 2)
                    if e:
                        y_acc.wait(pe, c, e)
                    else:
                        y_acc.wait(pe, c - 1)
                    for t in range(CH):
                        for k in range(KD):
                            ins = nc.tensor.matmul(ps[4 + t // 2][:, (t % 2) * D:(t % 2 + 1) * D],
                                                   HB[e % 2][:, k, t * P:(t + 1) * P], WOF[:, 2 * e + k, :],
                                                   start=k == 0, stop=k == KD - 1)
                        if t % 2:
                            ins.then_inc(o2_mm.sem, 1)

                def xf_transpose(c):
                    xf_norm.wait(pe, c)
                    y_init.wait(pe, c - 1)
                    for k in range(KD):
                        for t in range(CH):
                            ins = nc.tensor.transpose(ps[6 + k][:, t * P:(t + 1) * P], XF[:, t, k * P:(k + 1) * P],
                                                      ident[:, :])
                        ins.then_inc(xf_tr.sem, 1)

                def router(c, s):
                    xf_ev.wait(pe, c)
                    for t in range(CH):
                        for k in range(KD):
                            ins = nc.tensor.matmul(ps[7][:, t * NEXP:(t + 1) * NEXP], XFT[s][:, k, t * P:(t + 1) * P],
                                                   wr[:, k, :], start=k == 0, stop=k == KD - 1)
                    ins.then_inc(lg_mm.sem, 1)

                xf_transpose(0)
                router(0, 0)
                layer_1(0, 0, 0)

                def body(c, s, n, last):
                    for e in range(NEXP):
                        if e < NEXP - 1:
                            layer_1(c, s, e + 1)
                        elif not last:
                            layer_1(c + 1, 1 - s, 0)
                        if e == 0:
                            w_set.wait(pe, c)
                            for t in range(CH):
                                ins = nc.tensor.transpose(ps[6][0:NEXP, t * P:(t + 1) * P], WT8[s][:, t], ident[:, :])
                            ins.then_inc(w_tr.sem, 1)
                        layer_2(c, e)
                        if e == 0:
                            w_ev.wait(pe, c)
                            for t in range(CH):
                                ins = nc.tensor.matmul(ps[6 + t // 2][:, (t % 2) * D:(t % 2 + 1) * D],
                                                       wT[:, t * P:(t + 1) * P], bo[:, :], start=True, stop=True)
                            ins.then_inc(bo_mm.sem, 1)
                        else:
                            layer_3(c, e - 1)
                        if e == 5 and not last:
                            xf_transpose(c + 1)
                        if e == 6 and not last:
                            router(c + 1, 1 - s)
                    layer_3(c, NEXP - 1)
                ring(pe, NCH, 2, body)


_WEIGHTS = ["L0_gnn_W_src", "L0_gnn_W_dst", "L0_mix_Wq", "L0_mix_Wk", "L0_mix_Wv", "L0_mix_Wm", "L0_mix_W1", "L0_mix_W2",
            "L0_ffn_Wr", "L0_ffn_W1", "L0_ffn_W2", "L0_ffn_Wo", "L0_ffn_bo"]


def kernel(**inputs):
    import concourse.bacc as _bacc
    from concourse import mybir as _mybir
    from concourse.bass_utils import run_bass_kernel_spmd as _run

    g = {k: np.asarray(v) for k, v in inputs.items()}
    N, E = g["x"].shape[0], g["src"].shape[0]
    NP = -(-N // CT) * CT
    EP = -(-E // (P * GB)) * P * GB
    TE = EP // P
    KC = -(-TE // P)
    arrays = {name: np.ascontiguousarray(g[name]) for name in _WEIGHTS}
    arrays["x"] = np.concatenate([g["x"], np.zeros((NP - N, D), np.float32)])
    arrays["src"] = np.concatenate([g["src"], np.zeros(EP - E, np.int32)])
    dst = np.concatenate([g["dst"], np.full(EP - E, NP - 1, np.int32)])
    arrays["dst"] = dst
    edge = np.full(1, -1, np.int32)
    arrays["dst_prev"] = np.concatenate([edge, dst[:-1]])
    arrays["dst_next"] = np.concatenate([dst[1:], edge])
    ends = np.concatenate([dst.reshape(TE, P)[:, -1], np.full(KC * P - TE, 1 << 20, np.int32)])
    arrays["last_dst"] = np.ascontiguousarray(ends.reshape(KC, P).T)
    rows = [g["L0_gnn_bias"], g["L0_gnn_ln_gamma"], g["L0_gnn_ln_beta"], g["L0_gnn_prelu_w"], g["L0_mix_g2"], g["L0_mix_b2"],
            g["L0_ffn_br"], g["L0_gnn_att_src"].reshape(-1), g["L0_gnn_att_dst"].reshape(-1)]
    arrays["rows"] = np.ascontiguousarray(np.broadcast_to(np.concatenate(rows), (P, R_END)))
    cols = [g["L0_ffn_" + q].reshape(NEXP * KD, P) for q in ("b1", "g1", "be1", "m1", "v1", "b2", "g2", "be2", "m2", "v2")]
    cols += [g["L0_mix_g1"].reshape(KD, P), g["L0_mix_b1"].reshape(KD, P)]
    arrays["cols"] = np.ascontiguousarray(np.concatenate(cols).T)

    nc = _bacc.Bacc("TRN2", target_bir_lowering=False, num_devices=1)
    aps = {name: nc.dram_tensor("in_" + name, v.shape, _mybir.dt.from_np(v.dtype), kind="ExternalInput").ap()
           for name, v in arrays.items()}
    out = nc.dram_tensor("out_x", (NP, D), _mybir.dt.float32, kind="ExternalOutput").ap()
    build(nc, aps, out, N, E)
    r = _run(nc, [{"in_" + name: v for name, v in arrays.items()}], core_ids=[0])
    return r.results[0]["out_x"][:N]
```

```python
import numpy as np
import concourse.bass as bass
from concourse import mybir
from contextlib import ExitStack

P = 128
D = 256
HEADS = 4
KD = D // P
CH = 4
CT = CH * P
NEXP = 8
ATT_D = 32
BIG = 1.0e30
GU = 4
GB = 32
MW = D + HEADS
RECW = 10
LN_EPS = 1e-5
BN_EPS = 1e-3
ATT_EPS = 1e-6
MAGIC = 1597463007.0

C_H, C_AS, C_AD, C_K, C_V, C_END = 0, 256, 260, 264, 520, 776
R_BIAS, R_GAMMA, R_BETA, R_PRELU, R_G2, R_B2, R_BR, R_ATS, R_ATD, R_END = 0, 256, 512, 768, 1024, 1280, 1536, 1544, 1800, 2056
Q_B1, Q_G1, Q_BE1, Q_M1, Q_V1, Q_B2, Q_G2, Q_BE2, Q_M2, Q_V2, Q_MG, Q_MB, Q_END = [16 * i for i in range(11)] + [162, 164]


def ring(eng, total, slots, body, ahead=1):
    rounds = (total - ahead) // slots
    if rounds < 2:
        rounds = 1 if total > slots else 0
    for c in range(min(slots, total)):
        body(c, c, 0, c == total - 1)
    if rounds > 1:
        with eng.Fori(1, rounds) as i:
            for s in range(slots):
                body(i * slots + s, s, i, False)
    for c in range(max(rounds, 1) * slots, total):
        body(c, c % slots, c // slots, c == total - 1)


def used(eng, sem, per, n):
    if not (isinstance(n, int) and n == 0):
        eng.wait_ge(sem, per * n)


class Stage:

    def __init__(self, sem, per=1):
        self.sem, self.per = sem, per

    def wait(self, eng, turn, k=None):
        if not (isinstance(turn, int) and turn < 0):
            eng.wait_ge(self.sem, turn * self.per + (self.per if k is None else k))


def build(nc, a, out, N, E):
    f32, f32r, i32 = mybir.dt.float32, mybir.dt.float32r, mybir.dt.int32
    ALU, ACT, AX = mybir.AluOpType, mybir.ActivationFunctionType, mybir.AxisListType
    ET = mybir.EngineType

    NP = -(-N // CT) * CT
    NT, NCH = NP // P, NP // CT
    EP = -(-E // (P * GB)) * P * GB
    W = EP // P
    TE = W
    NB = -(-(TE + NT - 1) // GU)
    STEPS = NB * GU
    assert STEPS <= TE + NT
    KC = a["last_dst"].shape[1]
    NBLK = W // GB

    es = ExitStack()
    with es:
        def sb(name, shape, dt=f32):
            return es.enter_context(nc.sbuf_tensor(name, shape, dt))

        def sem(name):
            return es.enter_context(nc.semaphore(name))

        def dram(name, shape):
            return nc.dram_tensor(name, shape, f32, kind="Internal").ap()

        def stage(name, per=1):
            return Stage(sem(name), per)

        passed = {e: sem(f"passed_{e}") for e in ("sp", "dve", "pool")}

        def pass_on(eng, name):
            eng.sem_inc(passed[name], 1)

        class Region:
            def __init__(self, t):
                self.t, self.at = t, 0

            def take(self, *dims, dt=f32, parts=P):
                n = int(np.prod(dims))
                v = self.t[0:parts, self.at:self.at + n]
                self.at += -(-n // 8) * 8
                assert self.at <= self.t.shape[1], (self.at, self.t.shape)
                if dt != f32:
                    v = v.bitcast(dt)
                if len(dims) == 2:
                    v = v.rearrange("p (a b) -> p a b", b=dims[1])
                if len(dims) == 3:
                    v = v.rearrange("p (a b c) -> p a b c", b=dims[1], c=dims[2])
                return v

        h_tab = dram("h_tab", (NP, D))
        as_tab = dram("as_tab", (NP, HEADS))
        ad_tab = dram("ad_tab", (NP, HEADS))
        xnt_tab = dram("xnt_tab", (P, KD, NP))
        base_tab = dram("base_tab", (NP, D))
        rec_tab = dram("rec_tab", ((TE + 1) * P, RECW))
        acc_tab = dram("acc_tab", (P, NT * MW))

        ident = sb("ident", [P, P])
        iota_row = sb("iota_row", [P, P])
        rows = sb("rows", [P, R_END])
        cols = sb("cols", [P, Q_END])
        wr = sb("wr", [P, KD * NEXP])[:, :].rearrange("p (k e) -> p k e", k=KD)
        bo = sb("bo", [NEXP, D])
        bn = sb("bn", [P, 4 * 16])
        early = ExitStack()
        acc_t = early.enter_context(nc.sbuf_tensor("acc", [P, max(NT * MW, 25000)], f32))
        strip_t = early.enter_context(nc.sbuf_tensor("strips", [P, 12288], f32))
        work_t = early.enter_context(nc.sbuf_tensor("work", [P, 12088], f32))
        acc = acc_t[:, 0:NT * MW].rearrange("p (j c) -> p j c", c=MW)

        ps = [es.enter_context(nc.psum_tensor(f"ps{i}", [P, 512], f32)) for i in range(8)]

        def row(at, n=D):
            return rows[:, at:at + n]

        def rsqrt(dve, st, turn, k, y, v, vv, t, eps):
            def link(ins):
                nonlocal k
                k += 1
                ins.then_inc(st.sem, 1)
                st.wait(dve, turn, k)
            link(nc.vector.tensor_scalar(vv, v, 1.0, eps, ALU.mult, ALU.add))
            link(nc.vector.tensor_scalar(t.bitcast(i32), vv.bitcast(i32), 1, None, ALU.logical_shift_right))
            link(nc.vector.tensor_scalar(y.bitcast(i32), t.bitcast(i32), -1.0, MAGIC, ALU.mult, ALU.add))
            for _ in range(3):
                link(nc.vector.tensor_tensor(t, y, y, ALU.mult))
                link(nc.vector.scalar_tensor_tensor(t, t, -0.5, vv, ALU.mult, ALU.mult))
                link(nc.vector.scalar_tensor_tensor(y, t, 1.5, y, ALU.add, ALU.mult))
            return k

        RSQ = 12

        r1 = Region(acc_t)
        kvbd = r1.take(KD, P)
        ksbd = r1.take(KD, P)
        wq = r1.take(KD, D)
        wm = r1.take(KD, D)
        w1 = r1.take(2 * KD, 2 * D)
        w2 = r1.take(2 * KD, D)
        r2_from = r1.at
        wcat = r1.take(KD, C_END)
        wdst = r1.take(KD, D)
        fold = r1.take(2, KD, D)
        X = [r1.take(CH, D) for _ in range(2)]
        XN = [r1.take(CH, D) for _ in range(2)]
        XB = [r1.take(CH, D) for _ in range(2)]
        XT = [r1.take(KD, CT) for _ in range(2)]
        HS = [r1.take(CH, D) for _ in range(2)]
        KE = r1.take(CH, D)
        KR = r1.take(CH, D)
        KK = r1.take(CH, D)
        VX = r1.take(CH, KD, P + 1)
        zeros = r1.take(2 * (P + 1))
        stats = r1.take(CH, 6)
        mv = r1.take(CH, 2)
        rstd = r1.take(CH)
        tv = r1.take(CH)
        tt = r1.take(CH)
        p_kv = ps[6][:, 0:2 * (P + 1)].rearrange("p (g c) -> p g c", g=2)

        par_in, w_in, id_set, ones_set = sem("par_in"), sem("w_in"), sem("id_set"), sem("ones_set")
        fold_mul, fold_sum, id_zero = sem("fold_mul"), sem("fold_sum"), sem("id_zero")
        x_in = [sem(f"x_in{s}") for s in range(2)]
        x_stat, x_aggr, x_rs, x_norm, x_base = (stage("x_stat"), stage("x_aggr"), stage("x_rs", RSQ), stage("x_norm"),
                                                stage("x_base"))
        x_tr, xt_ev = stage("x_tr", 2), stage("xt_ev", 2)
        hk_mm, h_ev, k_act, k_dve, v_ev, kv_mm = (stage("hk_mm", CH), stage("h_ev", CH), stage("k_act", CH),
                                                  stage("k_dve", CH), stage("v_ev", CH), stage("kv_mm", CH))
        st_h = [sem(f"st_h{s}") for s in range(2)]
        kv_all, kv_cp, joined = sem("kv_all"), sem("kv_cp"), sem("joined")
        x_v = a["x"].rearrange("(c t p) d -> c p t d", t=CH, p=P)
        base_v = base_tab.rearrange("(c t p) d -> c p t d", t=CH, p=P)
        h_v = h_tab.rearrange("(c t p) d -> c p t d", t=CH, p=P)
        as_v = as_tab.rearrange("(c t p) d -> c p t d", t=CH, p=P)
        ad_v = ad_tab.rearrange("(c t p) d -> c p t d", t=CH, p=P)
        xnt_v = xnt_tab.rearrange("p k (c n) -> c p k n", n=CT)
        out_v = out.rearrange("(c t p) d -> c p t d", t=CH, p=P)

        def at(view, c):
            if isinstance(c, int):
                return view[c]
            return view[bass.ds(c, 1)].rearrange("o p k n -> (o p) k n")

        def weight(name):
            return a[name].rearrange("(k p) n -> p k n", p=P)

        LG = [r1.take(CH, 2 * HEADS) for _ in range(2)]
        l_in = [sem(f"l_in{s}") for s in range(2)]
        l_stat, l_aggr, l_rs, l_norm = stage("l_stat"), stage("l_aggr"), stage("l_rs", RSQ), stage("l_norm")
        l_tr, l_xt, l_mm, l_ev = stage("l_tr", 2), stage("l_xt", 2), stage("l_mm"), stage("l_ev")
        st_l = [sem(f"st_l{s}") for s in range(2)]

        with nc.Block() as block:
            @block.sync
            def _(sp):
                sp.dma_start(wcat[:, :, C_H:C_AS], weight("L0_gnn_W_src")).then_inc(w_in, 16)
                sp.dma_start(wdst, weight("L0_gnn_W_dst")).then_inc(w_in, 16)
                sp.dma_start(X[0], x_v[0]).then_inc(l_in[0], 16)
                sp.dma_start(rows[:, :], a["rows"]).then_inc(w_in, 16)
                sp.dma_start(wcat[:, :, C_K:C_V], weight("L0_mix_Wk")).then_inc(w_in, 16)
                sp.dma_start(wcat[:, :, C_V:C_END], weight("L0_mix_Wv")).then_inc(w_in, 16)
                for dst, src in ((cols[:, :], a["cols"]), (wr, weight("L0_ffn_Wr")), (bo[:, :], a["L0_ffn_bo"]),
                                 (wq, weight("L0_mix_Wq")), (wm, weight("L0_mix_Wm")), (w1, weight("L0_mix_W1")),
                                 (w2, weight("L0_mix_W2"))):
                    sp.dma_start(dst, src).then_inc(par_in, 16)

                def store_logits(c, s):
                    l_ev.wait(sp, c)
                    pass_on(sp, "sp")
                    sp.dma_start(at(as_v, c), LG[s][:, :, 0:HEADS]).then_inc(st_l[s], 16)
                    sp.dma_start(at(ad_v, c), LG[s][:, :, HEADS:2 * HEADS]).then_inc(st_l[s], 16)

                def body(c, s, n, last):
                    if not last:
                        l_norm.wait(sp, c - 1)
                        pass_on(sp, "sp")
                        sp.dma_start(X[1 - s], at(x_v, c + 1)).then_inc(l_in[1 - s], 16)
                    if not (isinstance(c, int) and c == 0):
                        store_logits(c - 1, 1 - s)
                ring(sp, NCH, 2, body)
                store_logits(NCH - 1, (NCH - 1) % 2)
                sp.wait_ge(st_l[0], 32 * ((NCH + 1) // 2))
                sp.wait_ge(st_l[1], 32 * (NCH // 2))
                sp.wait_ge(par_in, 16 * 7)

            @block.gpsimd
            def _(pool):
                nc.gpsimd.memset(ident[:, :], 0.0).then_inc(id_zero, 1)
                nc.gpsimd.iota(iota_row[:, :], pattern=[[1, P]], base=0, channel_multiplier=0,
                               allow_small_or_imprecise_dtypes=True)
                nc.gpsimd.memset(VX[:, :, :, P:P + 1], 1.0)
                nc.gpsimd.memset(zeros, 0.0).then_inc(ones_set, 1)
                pool.wait_ge(id_zero, 1)
                nc.gpsimd.affine_select(out=ident[:, :], in_=ident[:, :], compare_op=ALU.not_equal, fill=1.0, base=0,
                                        pattern=[[-1, P]], channel_multiplier=1).then_inc(id_set, 1)

            @block.vector
            def _(dve):
                dve.wait_ge(w_in, 80)
                for j, (w, r) in enumerate(((wcat[:, :, C_H:C_AS], R_ATS), (wdst, R_ATD))):
                    nc.vector.tensor_tensor(fold[:, j], w, row(r).unsqueeze(1).broadcast_to([P, KD, D]),
                                            ALU.mult).then_inc(fold_mul, 1)
                dve.wait_ge(fold_mul, 2)
                for j, col in enumerate((C_AS, C_AD)):
                    for k in range(KD):
                        nc.vector.tensor_reduce(wcat[:, k, col:col + HEADS],
                                                fold[:, j, k].rearrange("p (h c) -> p h c", h=HEADS), AX.X,
                                                ALU.add).then_inc(fold_sum, 1)

                def body(c, s, n, last):
                    dve.wait_ge(l_in[s], 16 * (n + 1))
                    for t in range(CH):
                        ins = nc.vector.bn_stats(stats[:, t], X[s][:, t])
                    ins.then_inc(l_stat.sem, 1)
                    l_stat.wait(dve, c)
                    pass_on(dve, "dve")
                    for t in range(CH):
                        ins = nc.vector.bn_aggr(mv[:, t], stats[:, t])
                    ins.then_inc(l_aggr.sem, 1)
                    l_aggr.wait(dve, c)
                    rsqrt(dve, l_rs, c, 0, rstd, mv[:, :, 1], tv, tt, LN_EPS)
                    l_tr.wait(dve, c - 2)
                    for t in range(CH):
                        ins = nc.vector.tensor_scalar(XN[s][:, t], X[s][:, t], mv[:, t, 0:1], rstd[:, t:t + 1],
                                                      ALU.subtract, ALU.mult)
                    ins.then_inc(l_norm.sem, 1)
                ring(dve, NCH, 2, body)
                dve.wait_ge(l_norm.sem, NCH)

            @block.scalar
            def _(act):

                def body(c, s, n, last):
                    l_mm.wait(act, c - 2)
                    for k in range(KD):
                        l_tr.wait(act, c, k + 1)
                        nc.scalar.activation(XT[s][:, k], ps[2 * s + k][:, :], ACT.Copy).then_inc(l_xt.sem, 1)
                    used(act, st_l[s], 32, n)
                    l_mm.wait(act, c)
                    nc.scalar.activation(LG[s].rearrange("p t h -> p (t h)"), ps[4 + s][:, 0:CH * 2 * HEADS], ACT.Copy
                                         ).then_inc(l_ev.sem, 1)
                ring(act, NCH, 2, body)

            @block.tensor
            def _(pe):
                pe.wait_ge(id_set, 1)
                pe.wait_ge(fold_sum, 4)

                def body(c, s, n, last):
                    l_norm.wait(pe, c)
                    l_xt.wait(pe, c - 2)
                    for k in range(KD):
                        for t in range(CH):
                            ins = nc.tensor.transpose(ps[2 * s + k][:, t * P:(t + 1) * P],
                                                      XN[s][:, t, k * P:(k + 1) * P], ident[:, :])
                        ins.then_inc(l_tr.sem, 1)
                    l_xt.wait(pe, c)
                    l_ev.wait(pe, c - 2)
                    for t in range(CH):
                        for k in range(KD):
                            ins = nc.tensor.matmul(ps[4 + s][:, t * 2 * HEADS:(t + 1) * 2 * HEADS],
                                                   XT[s][:, k, t * P:(t + 1) * P], wcat[:, k, C_AS:C_K],
                                                   start=k == 0, stop=k == KD - 1)
                    ins.then_inc(l_mm.sem, 1)
                ring(pe, NCH, 2, body)

        def project_sync(sp):
            for s in range(min(2, NCH)):
                sp.dma_start(X[s], x_v[s]).then_inc(x_in[s], 16)

            def body(c, s, n, last):
                x_base.wait(sp, c)
                pass_on(sp, "sp")
                sp.dma_start(at(base_v, c), XB[s]).then_inc(st_h[s], 16)
                if not (isinstance(c, int) and c + 2 >= NCH):
                    sp.dma_start(X[s], at(x_v, c + 2)).then_inc(x_in[s], 16)
                xt_ev.wait(sp, c)
                pass_on(sp, "sp")
                sp.dma_start(at(xnt_v, c), XT[s]).then_inc(st_h[s], 16)
                h_ev.wait(sp, c)
                pass_on(sp, "sp")
                sp.dma_start(at(h_v, c), HS[s]).then_inc(st_h[s], 16)
            ring(sp, NCH, 2, body, ahead=2)
            sp.wait_ge(st_h[0], 48 * ((NCH + 1) // 2))
            sp.wait_ge(st_h[1], 48 * (NCH // 2))
            sp.sem_inc(joined, 1)

        def project_vector(dve):
            def norm(c, s, n):
                dve.wait_ge(x_in[s], 16 * (n + 1))
                for t in range(CH):
                    ins = nc.vector.bn_stats(stats[:, t], X[s][:, t])
                ins.then_inc(x_stat.sem, 1)
                x_stat.wait(dve, c)
                pass_on(dve, "dve")
                for t in range(CH):
                    ins = nc.vector.bn_aggr(mv[:, t], stats[:, t])
                ins.then_inc(x_aggr.sem, 1)
                x_aggr.wait(dve, c)
                rsqrt(dve, x_rs, c, 0, rstd, mv[:, :, 1], tv, tt, LN_EPS)
                for t in range(CH):
                    ins = nc.vector.tensor_scalar(XN[s][:, t], X[s][:, t], mv[:, t, 0:1], rstd[:, t:t + 1],
                                                  ALU.subtract, ALU.mult)
                ins.then_inc(x_norm.sem, 1)
                x_norm.wait(dve, c)
                used(dve, st_h[s], 48, n)
                nc.vector.tensor_tensor(XB[s], X[s], XN[s], ALU.add).then_inc(x_base.sem, 1)

            norm(0, 0, 0)

            def body(c, s, n, last):
                if not last:
                    norm(c + 1, 1 - s, n + s)
                for t in range(CH):
                    k_act.wait(dve, c, t + 1)
                    kv_mm.wait(dve, c - 1, t + 1)
                    nc.vector.scalar_tensor_tensor(KK[:, t], KE[:, t], 1.0, KR[:, t], ALU.min,
                                                   ALU.add).then_inc(k_dve.sem, 1)
                    nc.vector.tensor_copy(VX[:, t, :, 0:P],
                                          ps[4 + t % 2][:, D:2 * D].rearrange("p (g c) -> p g c", g=KD)
                                          ).then_inc(v_ev.sem, 1)
            ring(dve, NCH, 2, body)
            nc.vector.memset(kvbd, 0.0)
            nc.vector.memset(ksbd, 0.0).then_inc(kv_cp, 1)
            dve.wait_ge(kv_cp, 1)
            dve.wait_ge(kv_all, 1)
            for g in range(KD):
                for b in range(P // ATT_D):
                    o = slice(b * ATT_D, (b + 1) * ATT_D)
                    nc.vector.tensor_copy(kvbd[o, g, o], p_kv[o, g, o])
                    nc.vector.tensor_copy(ksbd[o, g, o], p_kv[o, g, P:P + 1].broadcast_to([ATT_D, ATT_D])
                                          ).then_inc(kv_cp, 1)
            dve.wait_ge(kv_cp, 1 + KD * (P // ATT_D))
            dve.sem_inc(joined, 1)

        def project_scalar(act):

            def body(c, s, n, last):
                used(act, st_h[s], 48, n)
                hk_mm.wait(act, c - 1)
                for k in range(KD):
                    x_tr.wait(act, c, k + 1)
                    nc.scalar.activation(XT[s][:, k], ps[k][:, :], ACT.Copy).then_inc(xt_ev.sem, 1)
                for t in range(CH):
                    hk_mm.wait(act, c, t + 1)
                    nc.scalar.activation(HS[s][:, t], ps[2 + t % 2][:, 0:D], ACT.Copy).then_inc(h_ev.sem, 1)
                    k_dve.wait(act, c - 1, t + 1)
                    nc.scalar.activation(KE[:, t], ps[4 + t % 2][:, 0:D], ACT.Exp)
                    nc.scalar.activation(KR[:, t], ps[4 + t % 2][:, 0:D], ACT.Relu).then_inc(k_act.sem, 1)
            ring(act, NCH, 2, body)
            act.wait_ge(k_act.sem, CH * NCH)
            act.sem_inc(joined, 1)

        def project_tensor(pe):
            nc.tensor.matmul(ps[6][:, 0:2 * (P + 1)], zeros[:, 0:P], zeros, start=True, stop=False)

            def kv_sum(c, t, last):
                k_dve.wait(pe, c, t + 1)
                v_ev.wait(pe, c, t + 1)
                rows_in = P if not last else min(P, N - (c * CH + t) * P)
                final = last and N - (c * CH + t + 1) * P <= 0
                if rows_in <= 0:
                    nc.tensor.matmul(ps[7][:, 0:64], zeros[:, 0:P], zeros[:, 0:64], start=True,
                                     stop=True).then_inc(kv_mm.sem, 1)
                    return
                for g in range(KD):
                    ins = nc.tensor.matmul(p_kv[:, g, :], KK[0:rows_in, t, g * P:(g + 1) * P],
                                           VX[0:rows_in, t, g, :], start=False, stop=final and g == KD - 1)
                ins.then_inc(kv_mm.sem, 1)

            def body(c, s, n, last):
                x_norm.wait(pe, c)
                xt_ev.wait(pe, c - 1)
                for k in range(KD):
                    for t in range(CH):
                        ins = nc.tensor.transpose(ps[k][:, t * P:(t + 1) * P], XN[s][:, t, k * P:(k + 1) * P],
                                                  ident[:, :])
                    ins.then_inc(x_tr.sem, 1)
                xt_ev.wait(pe, c)
                for t in range(CH):
                    pc, pt = (c, t - 2) if t >= 2 else (c - 1, t + 2)
                    h_ev.wait(pe, pc, pt + 1)
                    k_act.wait(pe, pc, pt + 1)
                    v_ev.wait(pe, pc, pt + 1)
                    for lo, hi, bank in ((C_H, C_AS, 2), (C_K, C_END, 4)):
                        for k in range(KD):
                            ins = nc.tensor.matmul(ps[bank + t % 2][:, 0:hi - lo], XT[s][:, k, t * P:(t + 1) * P],
                                                   wcat[:, k, lo:hi], start=k == 0, stop=k == KD - 1)
                    ins.then_inc(hk_mm.sem, 1)
                    if t:
                        kv_sum(c, t - 1, last)
                kv_sum(c, CH - 1, last)
            ring(pe, NCH, 2, body)
            pe.wait_ge(kv_mm.sem, CH * NCH)
            pe.sem_inc(kv_all, 1)
            pe.sem_inc(joined, 1)

        r2 = Region(acc_t)
        r2.at = r2_from
        BX = [r2.take(CH, D) for _ in range(2)]
        BT = [r2.take(KD, CT) for _ in range(2)]
        QE, QR, QQ = r2.take(KD, CT), r2.take(KD, CT), r2.take(KD, CT)
        DR, MT = r2.take(KD, CT), r2.take(KD, CT)
        ML, MLT = r2.take(CH, D), r2.take(KD, CT)
        H1 = r2.take(2 * KD, CT)
        TM = r2.take(CH, D)
        bstats, bmv = r2.take(2, CH, 6), r2.take(2, CH, 2)
        brs, btv, btt = r2.take(2, CH), r2.take(2, CH), r2.take(2, CH)
        rw = Region(strip_t)
        s_strip = rw.take(W, HEADS)
        src_strip = rw.take(W, dt=i32)
        idx_blk = [rw.take(GB, dt=i32) for _ in range(2)]
        gat_blk = [rw.take(GB, HEADS) for _ in range(2)]
        rt = Region(work_t)
        neg_j = rt.take(STEPS)
        t_at = rt.at
        t_step = rt.take(STEPS, dt=i32, parts=1)
        j_step = work_t[32:33, t_at:t_at + STEPS].bitcast(i32)
        rt_from = rt.at
        kiota = rt.take(STEPS)
        cmp_f = [rt.take(512) for _ in range(2)]
        ones = rt.take(P)
        last_i, key = rt.take(KC, dt=i32), rt.take(KC)
        key_i, t_iota = rt.take(KC, dt=i32), rt.take(KC)

        bt_in = [sem(f"bt_in{s}") for s in range(2)]
        bx_in = [sem(f"bx_in{s}") for s in range(2)]
        q_mm, q_act, q_dve = stage("q_mm", 2), stage("q_act", 2), stage("q_dve", 2)
        nd_mm, n_e, n_r, n_m = stage("nd_mm", 2), stage("n_e", 2), stage("n_r", 2), stage("n_m", 2)
        m_mm, m_norm, m_tr, m_ev = stage("m_mm", CH), stage("m_norm"), stage("m_tr", 2), stage("m_ev", 2)
        u_mm, u_ev, o_mm, o_norm = stage("u_mm", 4), stage("u_ev", 4), stage("o_mm", CH), stage("o_norm")
        mo_st, mo_ag, mo_rs = stage("mo_st"), stage("mo_ag"), stage("mo_rs", RSQ)
        o_g, o_b, o_base = stage("o_g"), stage("o_b"), stage("o_base")
        st_b = [sem(f"st_b{s}") for s in range(2)]
        src_in, last_in = sem("src_in"), sem("last_in")
        idx_cp, gat_cp = stage("idx_cp"), stage("gat_cp")
        gat_in = [sem(f"gat_in{s}") for s in range(2)]
        io_set, key_set, cmp_set, cmp_mm, tab_set = sem("io_set"), sem("key_set"), sem("cmp_set"), sem("cmp_mm"), sem("tab_set")
        nseg = -(-STEPS // 512)

        with nc.Block() as block:
            @block.sync
            def _(sp):
                sp.dma_start(last_i, a["last_dst"]).then_inc(last_in, 16)
                project_sync(sp)
                sp.wait_ge(joined, 4)
                for s in range(min(2, NCH)):
                    sp.dma_start(BT[s], xnt_v[s]).then_inc(bt_in[s], 16)
                sp.dma_start(BX[0], base_v[0]).then_inc(bx_in[0], 16)

                def body(c, s, n, last):
                    u_mm.wait(sp, c)
                    pass_on(sp, "sp")
                    if not (isinstance(c, int) and c + 2 >= NCH):
                        sp.dma_start(BT[s], at(xnt_v, c + 2)).then_inc(bt_in[s], 16)
                    if not (isinstance(c, int) and c == 0):
                        o_base.wait(sp, c - 1)
                        pass_on(sp, "sp")
                        sp.dma_start(at(base_v, c - 1), BX[1 - s]).then_inc(st_b[1 - s], 16)
                        sp.wait_ge(st_b[1 - s], 16 * (n + s))
                        pass_on(sp, "sp")
                    if not last:
                        sp.dma_start(BX[1 - s], at(base_v, c + 1)).then_inc(bx_in[1 - s], 16)
                ring(sp, NCH, 2, body, ahead=2)
                o_base.wait(sp, NCH - 1)
                sp.dma_start(base_v[NCH - 1], BX[(NCH - 1) % 2]).then_inc(st_b[(NCH - 1) % 2], 16)
                sp.wait_ge(st_b[0], 16 * ((NCH + 1) // 2))
                sp.wait_ge(st_b[1], 16 * (NCH // 2))

            @block.gpsimd
            def _(pool):
                nc.gpsimd.iota(kiota, pattern=[[1, STEPS]], base=0, channel_multiplier=0,
                               allow_small_or_imprecise_dtypes=True).then_inc(io_set, 1)
                nc.gpsimd.iota(t_iota, pattern=[[P, KC]], base=0, channel_multiplier=1,
                               allow_small_or_imprecise_dtypes=True).then_inc(io_set, 1)
                nc.gpsimd.memset(ones, 1.0).then_inc(io_set, 1)
                pool.dma_start(src_strip, a["src"].rearrange("(p w) -> p w", p=P)).then_inc(src_in, 16)
                pool.wait_ge(src_in, 16)
                nc.gpsimd.tensor_copy(idx_blk[0], src_strip[:, 0:GB]).then_inc(idx_cp.sem, 1)

                def blk(v, b, n):
                    return v[:, bass.ds(b * n, n)] if not isinstance(b, int) else v[:, b * n:(b + 1) * n]

                s_flat = s_strip.rearrange("p w h -> p (w h)")

                def body(b, s, n, last):
                    idx_cp.wait(pool, b)
                    gat_cp.wait(pool, b - 2)
                    pass_on(pool, "pool")
                    for q in range(GB):
                        pool.indirect_dma_start(gat_blk[s][:, q], None, as_tab,
                                                bass.IndirectOffsetOnAxis(idx_blk[s][:, q:q + 1], 0)
                                                ).then_inc(gat_in[s], 16)
                        if q == GB // 2 and not (isinstance(b, int) and b == 0):
                            pool.wait_ge(gat_in[1 - s], 16 * GB * (n + s))
                            nc.gpsimd.tensor_copy(blk(s_flat, b - 1, GB * HEADS),
                                                  gat_blk[1 - s].rearrange("p q h -> p (q h)")).then_inc(gat_cp.sem, 1)
                        if q == GB // 2 and not last:
                            nc.gpsimd.tensor_copy(idx_blk[1 - s], blk(src_strip, b + 1, GB)).then_inc(idx_cp.sem, 1)
                ring(pool, NBLK, 2, body)
                fin = (NBLK - 1) % 2
                pool.wait_ge(gat_in[fin], 16 * GB * ((NBLK - 1) // 2 + 1))
                nc.gpsimd.tensor_copy(s_flat[:, (NBLK - 1) * GB * HEADS:NBLK * GB * HEADS],
                                      gat_blk[fin].rearrange("p q h -> p (q h)")).then_inc(gat_cp.sem, 1)

            @block.vector
            def _(dve):
                project_vector(dve)
                dve.wait_ge(joined, 4)
                dve.wait_ge(last_in, 16)
                dve.wait_ge(io_set, 3)
                nc.vector.tensor_scalar(key_i, last_i, 7, None, ALU.logical_shift_right).then_inc(key_set, 1)
                dve.wait_ge(key_set, 1)
                nc.vector.tensor_tensor(key, key_i, t_iota, ALU.add).then_inc(key_set, 1)
                dve.wait_ge(key_set, 2)
                for g in range(nseg):
                    w = min(512, STEPS - g * 512)
                    for k in range(KC):
                        i = g * KC + k
                        if i >= 2:
                            dve.wait_ge(cmp_mm, i - 1)
                        nc.vector.tensor_scalar(cmp_f[i % 2][:, 0:w], kiota[:, g * 512:g * 512 + w], key[:, k:k + 1],
                                                None, ALU.is_gt).then_inc(cmp_set, 1)
                    dve.wait_ge(cmp_mm, (g + 1) * KC)
                    seg = slice(g * 512, g * 512 + w)
                    nc.vector.tensor_copy(t_step[:, seg], ps[7][0:1, 0:w])
                    nc.vector.tensor_tensor(neg_j[:, seg], ps[7][:, 0:w], kiota[:, seg], ALU.subtract).then_inc(tab_set, 1)
                    dve.wait_ge(tab_set, 3 * g + 1)
                    nc.vector.tensor_scalar(j_step[:, seg], neg_j[32:33, seg], -1.0, None, ALU.mult).then_inc(tab_set, 1)
                    dve.wait_ge(tab_set, 3 * g + 2)
                    nc.vector.tensor_scalar(neg_j[:, seg], neg_j[:, seg], float(P), None, ALU.mult).then_inc(tab_set, 1)

                def q_elu(c):
                    for m in range(2):
                        q_act.wait(dve, c, m + 1)
                        nd_mm.wait(dve, c - 1)
                        nc.vector.scalar_tensor_tensor(QQ[:, m], QE[:, m], 1.0, QR[:, m], ALU.min,
                                                       ALU.add).then_inc(q_dve.sem, 1)

                def quotient(c):
                    for g in range(2):
                        n_e.wait(dve, c, g + 1)
                        nc.vector.reciprocal(DR[:, g], DR[:, g]).then_inc(n_r.sem, 1)
                        n_r.wait(dve, c, g + 1)
                        m_mm.wait(dve, c - 1)
                        nc.vector.tensor_tensor(MT[:, g], ps[2 + g][:, :], DR[:, g], ALU.mult).then_inc(n_m.sem, 1)

                def statistics(c, lo, hi):
                    for i in reversed(range(lo, hi)):
                        for t in range(CH):
                            if i:
                                o_mm.wait(dve, c - 1, (t | 1) + 1)
                            else:
                                m_mm.wait(dve, c, (t | 1) + 1)
                            ins = nc.vector.bn_stats(bstats[:, i, t], ps[(4, 6)[i] + t // 2][:, (t % 2) * D:(t % 2 + 1) * D])
                    ins.then_inc(mo_st.sem, 1)
                    mo_st.wait(dve, c)
                    pass_on(dve, "dve")
                    for i in range(lo, hi):
                        for t in range(CH):
                            ins = nc.vector.bn_aggr(bmv[:, i, t], bstats[:, i, t])
                    ins.then_inc(mo_ag.sem, 1)
                    mo_ag.wait(dve, c)
                    rsqrt(dve, mo_rs, c, 0, brs[:, lo:hi], bmv[:, lo:hi, :, 1], btv[:, lo:hi], btt[:, lo:hi], LN_EPS)

                def m_apply(c):
                    for t in range(CH):
                        ins = nc.vector.tensor_scalar(ML[:, t], ps[4 + t // 2][:, (t % 2) * D:(t % 2 + 1) * D],
                                                      bmv[:, 0, t, 0:1], brs[:, 0, t:t + 1], ALU.subtract, ALU.mult)
                    ins.then_inc(m_norm.sem, 1)

                def o_apply(c):
                    for t in range(CH):
                        ins = nc.vector.tensor_scalar(TM[:, t], ps[6 + t // 2][:, (t % 2) * D:(t % 2 + 1) * D],
                                                      bmv[:, 1, t, 0:1], brs[:, 1, t:t + 1], ALU.subtract, ALU.mult)
                    ins.then_inc(o_norm.sem, 1)

                def o_finish(c, s, uses):
                    o_norm.wait(dve, c)
                    nc.vector.tensor_tensor(TM, TM, row(R_G2).unsqueeze(1).broadcast_to([P, CH, D]),
                                            ALU.mult).then_inc(o_g.sem, 1)
                    o_g.wait(dve, c)
                    nc.vector.tensor_tensor(TM, TM, row(R_B2).unsqueeze(1).broadcast_to([P, CH, D]),
                                            ALU.add).then_inc(o_b.sem, 1)
                    o_b.wait(dve, c)
                    dve.wait_ge(bx_in[s], 16 * uses)
                    nc.vector.tensor_tensor(BX[s], BX[s], TM, ALU.add).then_inc(o_base.sem, 1)

                q_elu(0)
                quotient(0)

                def body(c, s, n, last):
                    first = isinstance(c, int) and c == 0
                    statistics(c, 0, 1 if first else 2)
                    m_apply(c)
                    if not last:
                        q_elu(c + 1)
                    if not first:
                        o_apply(c - 1)
                    if not last:
                        quotient(c + 1)
                    if not first:
                        o_finish(c - 1, 1 - s, n + s)
                ring(dve, NCH, 2, body)
                statistics(NCH, 1, 2)
                o_apply(NCH - 1)
                o_finish(NCH - 1, (NCH - 1) % 2, (NCH - 1) // 2 + 1)

            @block.scalar
            def _(act):
                project_scalar(act)
                act.wait_ge(joined, 4)

                def q_parts(c):
                    for m in range(2):
                        q_mm.wait(act, c, m + 1)
                        q_dve.wait(act, c - 1, m + 1)
                        nc.scalar.activation(QE[:, m], ps[m][:, :], ACT.Exp)
                        nc.scalar.activation(QR[:, m], ps[m][:, :], ACT.Relu).then_inc(q_act.sem, 1)

                def denominator(c):
                    for g in range(2):
                        nd_mm.wait(act, c, g + 1)
                        n_m.wait(act, c - 1, g + 1)
                        nc.scalar.activation(DR[:, g], ps[6 + g][:, :], ACT.Copy, bias=ATT_EPS).then_inc(n_e.sem, 1)

                q_parts(0)
                denominator(0)

                def body(c, s, n, last):
                    if not last:
                        q_parts(c + 1)
                    for k in range(KD):
                        m_tr.wait(act, c, k + 1)
                        u_mm.wait(act, c - 1)
                        nc.scalar.activation(MLT[:, k], ps[4 + k][:, :], ACT.Identity, scale=cols[:, Q_MG + k:Q_MG + k + 1],
                                             bias=cols[:, Q_MB + k:Q_MB + k + 1]).then_inc(m_ev.sem, 1)
                    if not last:
                        denominator(c + 1)
                    for m in range(4):
                        u_mm.wait(act, c, m + 1)
                        o_mm.wait(act, c - 1)
                        nc.scalar.activation(H1[:, m], ps[(0, 1, 4, 5)[m]][:, :], ACT.Relu).then_inc(u_ev.sem, 1)
                ring(act, NCH, 2, body)

            @block.tensor
            def _(pe):
                project_tensor(pe)
                pe.wait_ge(joined, 4)
                for g in range(nseg):
                    w = min(512, STEPS - g * 512)
                    if g:
                        pe.wait_ge(tab_set, 3 * g)
                    for k in range(KC):
                        i = g * KC + k
                        pe.wait_ge(cmp_set, i + 1)
                        nc.tensor.matmul(ps[7][:, 0:w], ones, cmp_f[i % 2][:, 0:w], start=k == 0,
                                         stop=k == KC - 1).then_inc(cmp_mm, 1)

                def q_product(c, s, uses):
                    pe.wait_ge(bt_in[s], 16 * uses)
                    for m in range(2):
                        for k in range(KD):
                            ins = nc.tensor.matmul(ps[m][:, :], wq[:, k, m * P:(m + 1) * P], BT[s][:, k, :],
                                                   start=k == 0, stop=k == KD - 1)
                        ins.then_inc(q_mm.sem, 1)

                def attend(c):
                    for g in range(2):
                        q_dve.wait(pe, c, g + 1)
                        nc.tensor.matmul(ps[2 + g][:, :], kvbd[:, g], QQ[:, g], start=True, stop=True)
                        nc.tensor.matmul(ps[6 + g][:, :], ksbd[:, g], QQ[:, g], start=True, stop=True).then_inc(nd_mm.sem, 1)

                q_product(0, 0, 1)
                attend(0)

                def body(c, s, n, last):
                    n_m.wait(pe, c)
                    u_ev.wait(pe, c - 1)
                    for t in range(CH):
                        for k in range(KD):
                            ins = nc.tensor.matmul(ps[4 + t // 2][:, (t % 2) * D:(t % 2 + 1) * D],
                                                   MT[:, k, t * P:(t + 1) * P], wm[:, k, :], start=k == 0, stop=k == KD - 1)
                        ins.then_inc(m_mm.sem, 1)
                    if not last:
                        q_product(c + 1, 1 - s, n + s + 1)
                    m_norm.wait(pe, c)
                    for k in range(KD):
                        for t in range(CH):
                            ins = nc.tensor.transpose(ps[4 + k][:, t * P:(t + 1) * P], ML[:, t, k * P:(k + 1) * P],
                                                      ident[:, :])
                        ins.then_inc(m_tr.sem, 1)
                    o_norm.wait(pe, c - 1)
                    if not last:
                        attend(c + 1)
                        q_act.wait(pe, c + 1)
                    m_ev.wait(pe, c)
                    for m in range(4):
                        for k in range(4):
                            rhs = BT[s][:, k, :] if k < 2 else MLT[:, k - 2, :]
                            ins = nc.tensor.matmul(ps[(0, 1, 4, 5)[m]][:, :], w1[:, k, m * P:(m + 1) * P], rhs,
                                                   start=k == 0, stop=k == 3)
                        ins.then_inc(u_mm.sem, 1)
                    u_ev.wait(pe, c)
                    if not last:
                        n_e.wait(pe, c + 1)
                    for t in range(CH):
                        for k in range(4):
                            ins = nc.tensor.matmul(ps[6 + t // 2][:, (t % 2) * D:(t % 2 + 1) * D],
                                                   H1[:, k, t * P:(t + 1) * P], w2[:, k, :], start=k == 0, stop=k == 3)
                        ins.then_inc(o_mm.sem, 1)
                ring(pe, NCH, 2, body)

        r3 = Region(acc_t)
        rec = r3.take(W, RECW)
        gap_prev, gap_next = r3.take(W), r3.take(W)
        run = r3.take(W)
        rw3 = Region(strip_t)
        rw3.at = rw.at
        dst_i, oth_i = r3.take(W, dt=i32), rw3.take(W, dt=i32)
        edge_end = r3.take(3, HEADS)
        lt = r3.take(3, P, parts=HEADS)
        carry = r3.take(HEADS, P + 1, parts=HEADS)
        padrow = r3.take(RECW)
        s3_in, s3_gap, s3_scan, s3_tr, s3_car, s3_cc, s3_rec, s3_st, s3_pad = (
            sem("s3_in"), sem("s3_gap"), sem("s3_scan"), sem("s3_tr"), sem("s3_car"),
            sem("s3_cc"), sem("s3_rec"), sem("s3_st"), sem("s3_pad"))
        s3_end = sem("s3_end")
        strip = lambda name: a[name].rearrange("(p w) -> p w", p=P)

        with nc.Block() as block:
            @block.sync
            def _(sp):
                sp.dma_start(dst_i, strip("dst")).then_inc(s3_in, 16)
                sp.dma_start(oth_i, strip("dst_prev")).then_inc(s3_in, 16)
                sp.wait_ge(s3_gap, 1)
                sp.dma_start(oth_i, strip("dst_next")).then_inc(s3_in, 16)
                sp.wait_ge(s3_pad, 3)
                sp.dma_start(rec_tab[TE * P:(TE + 1) * P, :], padrow).then_inc(s3_st, 16)
                sp.wait_ge(s3_rec, 1)
                sp.dma_start(rec_tab[0:EP, :].rearrange("(p w) r -> p w r", p=P), rec).then_inc(s3_st, 16)
                sp.wait_ge(s3_st, 32)

            @block.scalar
            def _(act):
                act.wait_ge(s3_in, 48)
                nc.scalar.activation(rec[:, :, 1], dst_i, ACT.Copy)
                nc.scalar.activation(rec[:, :, 2:6], s_strip, ACT.Copy).then_inc(s3_cc, 1)

            @block.gpsimd
            def _(pool):
                nc.gpsimd.tensor_copy(rec[:, :, 0:1].bitcast(i32).rearrange("p w o -> p (w o)"), src_strip)
                nc.gpsimd.memset(padrow, 0.0).then_inc(s3_pad, 1)
                pool.wait_ge(s3_pad, 1)
                nc.gpsimd.memset(padrow[:, 1:2], -1.0).then_inc(s3_pad, 2)

            @block.vector
            def _(dve):
                v = [0]

                def link(ins):
                    v[0] += 1
                    ins.then_inc(s3_scan, 1)
                    dve.wait_ge(s3_scan, v[0])

                dve.wait_ge(s3_in, 32)
                nc.vector.tensor_tensor(gap_prev, dst_i, oth_i, ALU.not_equal).then_inc(s3_gap, 1)
                dve.wait_ge(s3_gap, 1)
                link(nc.vector.tensor_scalar(gap_prev, gap_prev, -BIG, None, ALU.mult))
                dve.wait_ge(s3_in, 48)
                link(nc.vector.tensor_tensor(gap_next, dst_i, oth_i, ALU.not_equal))
                link(nc.vector.tensor_scalar(gap_next, gap_next, -BIG, None, ALU.mult))

                def carried(d, gap):
                    nc.vector.tensor_reduce(edge_end[:, 1], gap.unsqueeze(1).broadcast_to([P, HEADS, W]), AX.X,
                                            ALU.min).then_inc(s3_end, 1)
                    dve.wait_ge(s3_tr, 2 * d + 1)
                    link(nc.vector.tensor_copy(lt[:, 0:2], ps[0][0:HEADS, 0:2 * P].rearrange("p (a b) -> p a b", a=2)))
                    cr = carry[:, d]
                    link(nc.vector.memset(cr, -BIG))
                    if d == 0:
                        link(nc.vector.tensor_tensor_scan(cr[:, 1:P + 1], lt[:, 1], lt[:, 0], -BIG, ALU.add, ALU.max))
                    else:
                        link(nc.vector.tensor_tensor_scan(cr[:, 0:P][:, ::-1], lt[:, 1][:, ::-1], lt[:, 0][:, ::-1],
                                                          -BIG, ALU.add, ALU.max))
                    dve.sem_inc(s3_car, 1)
                    dve.wait_ge(s3_tr, 2 * d + 2)
                    link(nc.vector.tensor_copy(edge_end[:, 2], ps[1][:, 0:HEADS]))

                for h in range(HEADS):
                    link(nc.vector.tensor_tensor_scan(run, gap_prev, s_strip[:, :, h], -BIG, ALU.add, ALU.max))
                    link(nc.vector.tensor_copy(edge_end[:, 0, h:h + 1], run[:, W - 1:W]))
                carried(0, gap_prev)
                for h in range(HEADS):
                    link(nc.vector.tensor_tensor_scan(rec[:, :, 6 + h], gap_prev, s_strip[:, :, h],
                                                      edge_end[:, 2, h:h + 1], ALU.add, ALU.max))
                for h in range(HEADS):
                    link(nc.vector.tensor_tensor_scan(run[:, ::-1], gap_next[:, ::-1], rec[:, :, 6 + h][:, ::-1],
                                                      -BIG, ALU.add, ALU.max))
                    link(nc.vector.tensor_copy(edge_end[:, 0, h:h + 1], run[:, 0:1]))
                carried(1, gap_next)
                for h in range(HEADS):
                    link(nc.vector.tensor_tensor_scan(run[:, ::-1], gap_next[:, ::-1], rec[:, :, 6 + h][:, ::-1],
                                                      edge_end[:, 2, h:h + 1], ALU.add, ALU.max))
                    link(nc.vector.tensor_copy(rec[:, :, 6 + h], run))
                dve.wait_ge(s3_cc, 1)
                dve.wait_ge(s3_pad, 3)
                dve.sem_inc(s3_rec, 1)

            @block.tensor
            def _(pe):
                for d in range(2):
                    pe.wait_ge(s3_end, d + 1)
                    for j in range(2):
                        ins = nc.tensor.transpose(ps[0][0:HEADS, j * P:(j + 1) * P], edge_end[:, j], ident[:, :])
                    ins.then_inc(s3_tr, 1)
                    pe.wait_ge(s3_car, d + 1)
                    src = carry[:, 0, 0:P] if d == 0 else carry[:, 1, 1:P + 1]
                    nc.tensor.transpose(ps[1][:, 0:HEADS], src, ident[0:HEADS, 0:HEADS]).then_inc(s3_tr, 1)

        r4 = Region(work_t)
        r4.at = rt_from
        RECS = [r4.take(GU, RECW) for _ in range(4)]
        ad_all = r4.take(NT, HEADS)
        G = [r4.take(GU, MW) for _ in range(4)]
        S = [r4.take(GU, P) for _ in range(4)]
        ST = r4.take(GU, P)
        dr = r4.take(GU)
        zz, lk = r4.take(GU, 2, HEADS), r4.take(GU, 2, HEADS)
        df = r4.take(GU, HEADS)
        bnt = [r4.take(16) for _ in range(3)]
        rec_in = [sem(f"rec_in{s}") for s in range(4)]
        ad_in = sem("ad_in")
        g_in = [sem(f"g_in{s}") for s in range(4)]
        dr_set, s_set, t_mm, st_ev, d_mm = stage("dr_set"), stage("s_set", GU), stage("t_mm"), stage("st_ev"), stage("d_mm")
        z_set, l_set, p_df, p_exp, msg_set = stage("z_set"), stage("l_set"), stage("p_df"), stage("p_exp"), stage("msg_set")
        g_mm, acc_add = stage("g_mm", GU), stage("acc_add", GU)
        acc_zero, acc_out, bn_st = sem("acc_zero"), sem("acc_out"), stage("bn_st", 2 * (RSQ + 2))
        rec_v = rec_tab.rearrange("(t p) r -> t p r", p=P)

        def more(b, by):
            return not (isinstance(b, int) and b + by >= NB)

        BOUND = "the tables hold edge tiles up to TE and node tiles below NT by their making"

        def step_values(engine, table, b, most):
            lo = b * GU
            sl = table[:, lo:lo + GU] if isinstance(b, int) else table[:, bass.ds(lo, GU)]
            return nc.values_load_multi_w_load_instructions(sl, engines=[engine], min_val=0, max_val=most,
                                                            skip_runtime_bounds_check_because=BOUND)[1]

        with nc.Block() as block:
            @block.sync
            def _(sp):
                def body(b, s, n, last):
                    ts = step_values(ET.SP, t_step, b, TE)
                    msg_set.wait(sp, b - 4)
                    pass_on(sp, "sp")
                    for u in range(GU):
                        sp.dma_start(RECS[s][:, u], rec_v[bass.ds(ts[u], 1)].rearrange("o p r -> (o p) r")
                                     ).then_inc(rec_in[s], 16)
                sp.dma_start(ad_all, ad_tab.rearrange("(t p) r -> p t r", p=P)).then_inc(ad_in, 16)
                ring(sp, NB, 4, body)
                sp.wait_ge(acc_add.sem, GU * NB)
                for q in range(4):
                    cut = slice(q * NT // 4 * MW, (q + 1) * NT // 4 * MW)
                    sp.dma_start(acc_tab[:, cut], acc_t[:, cut]).then_inc(acc_out, 16)
                sp.wait_ge(acc_out, 16 * 4)

            @block.gpsimd
            def _(pool):
                def body(b, s, n, last):
                    pool.wait_ge(rec_in[s], 64 * (n + 1))
                    g_mm.wait(pool, b - 4)
                    pass_on(pool, "pool")
                    for u in range(GU):
                        pool.indirect_dma_start(G[s][:, u, 0:D], None, h_tab,
                                                bass.IndirectOffsetOnAxis(RECS[s][:, u, 0:1].bitcast(i32), 0)
                                                ).then_inc(g_in[s], 16)
                ring(pool, NB, 4, body)

            @block.vector
            def _(dve):
                def relative(b, s, n):
                    dve.wait_ge(rec_in[s], 64 * (n + 1))
                    s_set.wait(dve, b - 1)
                    nj = neg_j[:, b * GU:(b + 1) * GU] if isinstance(b, int) else neg_j[:, bass.ds(b * GU, GU)]
                    nc.vector.tensor_tensor(dr, RECS[s][:, :, 1], nj, ALU.add).then_inc(dr_set.sem, 1)

                def onehot(b, s, u):
                    dr_set.wait(dve, b)
                    nc.vector.tensor_scalar(S[s][:, u], iota_row[:, :], dr[:, u:u + 1], None, ALU.is_equal
                                            ).then_inc(s_set.sem, 1)

                def logits(b, s):
                    d_mm.wait(dve, b)
                    d_e = ps[5][:, 0:GU * HEADS].rearrange("p (u h) -> p u h", u=GU)
                    nc.vector.tensor_tensor(zz, RECS[s][:, :, 2:10].rearrange("p u (a h) -> p u a h", a=2),
                                            d_e.unsqueeze(2).broadcast_to([P, GU, 2, HEADS]), ALU.add
                                            ).then_inc(z_set.sem, 1)

                def leaky(b):
                    z_set.wait(dve, b)
                    zf, lf = zz.rearrange("p u a h -> p (u a h)"), lk.rearrange("p u a h -> p (u a h)")
                    nc.vector.scalar_tensor_tensor(lf, zf, 0.2, zf, ALU.mult, ALU.max).then_inc(l_set.sem, 1)

                def difference(b):
                    l_set.wait(dve, b)
                    nc.vector.tensor_tensor(df, lk[:, :, 0], lk[:, :, 1], ALU.subtract).then_inc(p_df.sem, 1)

                def message(b, s, n):
                    p_exp.wait(dve, b)
                    dve.wait_ge(g_in[s], 64 * (n + 1))
                    msg = G[s][:, :, 0:D].rearrange("p u (h c) -> p u h c", h=HEADS)
                    nc.vector.tensor_tensor(msg, msg, G[s][:, :, D:MW].unsqueeze(3).broadcast_to([P, GU, HEADS, D // HEADS]),
                                            ALU.mult).then_inc(msg_set.sem, 1)

                def add(b, u, j):
                    g_mm.wait(dve, b, u + 1)
                    if u:
                        acc_add.wait(dve, b, u)
                    else:
                        acc_add.wait(dve, b - 1)
                        if isinstance(b, int) and b == 0:
                            dve.wait_ge(acc_zero, 2)
                    aj = acc[:, bass.ds(j, 1)].rearrange("p o c -> p (o c)")
                    nc.vector.tensor_tensor(aj, aj, ps[u][:, 0:MW], ALU.add).then_inc(acc_add.sem, 1)

                for b in range(3):
                    relative(b, b, 0)
                    for u in range(GU):
                        onehot(b, b, u)
                for b in range(2):
                    logits(b, b)
                    leaky(b)
                    difference(b)
                    if b == 0:
                        message(0, 0, 0)
                half = NT * MW // 2
                nc.vector.memset(acc_t[:, 0:half], 0.0).then_inc(acc_zero, 1)
                k = 0
                for j, (qb, qg, qbe, qm, qv) in enumerate(((Q_B1, Q_G1, Q_BE1, Q_M1, Q_V1), (Q_B2, Q_G2, Q_BE2, Q_M2, Q_V2))):
                    sc, of = bn[:, 32 * j:32 * j + 16], bn[:, 32 * j + 16:32 * j + 32]
                    col = lambda q: cols[:, q:q + 16]
                    k = rsqrt(dve, bn_st, 0, k, sc, col(qv), bnt[0], bnt[1], BN_EPS)
                    nc.vector.tensor_tensor(sc, sc, col(qg), ALU.mult)
                    nc.vector.tensor_tensor(bnt[2], col(qb), col(qm), ALU.subtract).then_inc(bn_st.sem, 1)
                    bn_st.wait(dve, 0, k + 1)
                    nc.vector.tensor_tensor(bnt[2], bnt[2], sc, ALU.mult).then_inc(bn_st.sem, 1)
                    bn_st.wait(dve, 0, k + 2)
                    k += 2
                    nc.vector.tensor_tensor(of, bnt[2], col(qbe), ALU.add)

                def body(b, s, n, last):
                    s2, s3, n3 = (s + 2) % 4, (s + 3) % 4, n + (s >= 1)
                    if more(b, 1):
                        message(b + 1, (s + 1) % 4, n + (s >= 3))
                    js = step_values(ET.DVE, j_step, b, NT - 1)
                    add(b, 0, js[0])
                    if more(b, 3):
                        relative(b + 3, s3, n3)
                        onehot(b + 3, s3, 0)
                        onehot(b + 3, s3, 1)
                    add(b, 1, js[1])
                    if more(b, 2):
                        logits(b + 2, s2)
                    if more(b, 3):
                        onehot(b + 3, s3, 2)
                    if more(b, 2):
                        leaky(b + 2)
                    add(b, 2, js[2])
                    if more(b, 3):
                        onehot(b + 3, s3, 3)
                    if more(b, 2):
                        difference(b + 2)
                    add(b, 3, js[3])
                ring(dve, NB, 4, body, ahead=3)

            @block.scalar
            def _(act):
                half = NT * MW // 2
                nc.scalar.memzero(acc_t[:, half:NT * MW]).then_inc(acc_zero, 1)

                def transposed(b):
                    t_mm.wait(act, b)
                    d_mm.wait(act, b - 1)
                    nc.scalar.activation(ST.rearrange("p u n -> p (u n)"), ps[4][:, :], ACT.Copy).then_inc(st_ev.sem, 1)

                def exponent(b, s):
                    p_df.wait(act, b)
                    g_mm.wait(act, b - 4)
                    nc.scalar.activation(G[s][:, :, D:MW], df, ACT.Exp).then_inc(p_exp.sem, 1)
                for b in range(2):
                    transposed(b)
                    exponent(b, b)

                def body(b, s, n, last):
                    if more(b, 2):
                        transposed(b + 2)
                        exponent(b + 2, (s + 2) % 4)
                ring(act, NB, 4, body, ahead=3)

            @block.tensor
            def _(pe):
                def transpose(b, s):
                    s_set.wait(pe, b)
                    st_ev.wait(pe, b - 1)
                    for u in range(GU):
                        ins = nc.tensor.transpose(ps[4][:, u * P:(u + 1) * P], S[s][:, u], ident[:, :])
                    ins.then_inc(t_mm.sem, 1)

                def dst_logits(b, js):
                    st_ev.wait(pe, b)
                    z_set.wait(pe, b - 1)
                    for u in range(GU):
                        ins = nc.tensor.matmul(ps[5][:, u * HEADS:(u + 1) * HEADS], ST[:, u],
                                               ad_all[:, bass.ds(js[u], 1)].rearrange("p o h -> p (o h)"),
                                               start=True, stop=True)
                    ins.then_inc(d_mm.sem, 1)
                pe.wait_ge(ad_in, 16)
                for b in range(2):
                    transpose(b, b)
                    dst_logits(b, step_values(ET.PE, j_step, b, NT - 1))

                def body(b, s, n, last):
                    if more(b, 2):
                        js = step_values(ET.PE, j_step, b + 2, NT - 1)
                    msg_set.wait(pe, b)
                    for u in range(GU):
                        acc_add.wait(pe, b - 1, u + 1)
                        nc.tensor.matmul(ps[u][:, 0:MW], S[s][:, u], G[s][:, u], start=True,
                                         stop=True).then_inc(g_mm.sem, 1)
                        if u == 0 and more(b, 2):
                            transpose(b + 2, (s + 2) % 4)
                        if u == 1 and more(b, 2):
                            dst_logits(b + 2, js)
                ring(pe, NB, 4, body, ahead=3)

        early.close()
        WHI = [sb(f"w_hi{i}", [P, NEXP * KD * D], f32r) for i in range(3)]
        WLO = [sb(f"w_lo{i}", [P, NEXP * KD * D], f32r) for i in range(3)]
        WP = 1024
        pieces = [(i, p * WP) for i in range(3) for p in range(NEXP * KD * D // WP)]
        WR = [sb(f"w_raw{s}", [P, WP]) for s in range(2)]

        def pair(name):
            return [[sb(f"{name}_{half}{s}", [P, KD * CT], f32r)[:, :].rearrange("p (k n) -> p k n", k=KD)
                     for s in range(2)] for half in ("hi", "lo")]
        (XHI, XLO), (AHI, ALO), (BHI, BLO) = pair("x"), pair("a"), pair("b")
        exp_t = sb("exp", [P, 10400])
        r5 = Region(exp_t)
        AC = [r5.take(CH, MW) for _ in range(2)]
        XFR, AR, BR = r5.take(KD, CT), r5.take(KD, CT), r5.take(KD, CT)
        Y = [r5.take(CH, D) for _ in range(2)]
        O, XF = r5.take(CH, D), r5.take(CH, D)
        rden = r5.take(CH, HEADS)
        lg, ex = r5.take(CH, NEXP), r5.take(CH, NEXP)
        WT8 = [r5.take(CH, NEXP) for _ in range(2)]
        mx, sm = r5.take(CH), r5.take(CH)
        wT = r5.take(CT, parts=NEXP)
        cst, cmv = r5.take(2, CH, 6), r5.take(2, CH, 2)
        crs, ctv, ctt = r5.take(2, CH), r5.take(2, CH), r5.take(2, CH)
        y_in = [sem(f"y_in{s}") for s in range(2)]
        st_o = [sem(f"st_o{s}") for s in range(2)]
        prep = stage("prep", 14)
        c_rs, xf_tr, xf_ev, lg_mm, ex_act = stage("c_rs", 2 * RSQ), stage("xf_tr", 2), stage("xf_ev", 2), stage("lg_mm"), stage("ex_act")
        xf_norm, lg_sub, w_set, w_tr, w_ev, bo_mm, y_init = (stage("xf_norm"), stage("lg_sub"), stage("w_set"),
                                                             stage("w_tr"), stage("w_ev"), stage("bo_mm"), stage("y_init"))
        lg_st = stage("lg_st", 4)
        a_mm, a_ev, b_mm, b_ev = (stage(x, 2 * NEXP) for x in ("a_mm", "a_ev", "b_mm", "b_ev"))
        o2_mm, y_acc = stage("o2_mm", NEXP * 2), stage("y_acc", NEXP)
        xf_lo, a_lo, b_lo = stage("xf_lo"), stage("a_lo", 2 * NEXP), stage("b_lo", 2 * NEXP)
        ac_in = [sem(f"ac_in{s}") for s in range(2)]
        wr_in = [sem(f"wr_in{s}") for s in range(2)]
        w_hi, w_lo = sem("w_hi"), sem("w_lo")
        acc_v = acc_tab.rearrange("p (c x) -> c p x", x=CH * MW)

        def acc_at(c):
            return acc_v[c] if isinstance(c, int) else acc_v[bass.ds(c, 1)].rearrange("o p x -> (o p) x")

        def flat(v):
            return v.rearrange("p a b -> p (a b)")

        with nc.Block() as block:
            @block.sync
            def _(sp):
                for s in range(min(2, NCH)):
                    sp.dma_start(flat(AC[s]), acc_at(s)).then_inc(ac_in[s], 16)
                sp.dma_start(Y[0], base_v[0]).then_inc(y_in[0], 16)
                for i, (w, lo) in enumerate(pieces):
                    if i >= 2:
                        sp.wait_ge(w_hi, i - 1)
                        sp.wait_ge(w_lo, i - 1)
                    src = a[("L0_ffn_W1", "L0_ffn_W2", "L0_ffn_Wo")[w]].rearrange("e (k p) n -> p (e k) n", p=P)
                    sp.dma_start(WR[i % 2][:, :].rearrange("p (b n) -> p b n", n=D),
                                 src[:, lo // D:(lo + WP) // D, :]).then_inc(wr_in[i % 2], 16)

                def body(c, s, n, last):
                    if not (isinstance(c, int) and c + 2 >= NCH):
                        prep.wait(sp, c, 3)
                        pass_on(sp, "sp")
                        sp.dma_start(flat(AC[s]), acc_at(c + 2)).then_inc(ac_in[s], 16)
                    if not last:
                        used(sp, st_o[1 - s], 16, n + s)
                        pass_on(sp, "sp")
                        sp.dma_start(Y[1 - s], at(base_v, c + 1)).then_inc(y_in[1 - s], 16)
                    y_acc.wait(sp, c)
                    pass_on(sp, "sp")
                    sp.dma_start(at(out_v, c), Y[s]).then_inc(st_o[s], 16)
                ring(sp, NCH, 2, body, ahead=2)
                sp.wait_ge(st_o[0], 16 * ((NCH + 1) // 2))
                sp.wait_ge(st_o[1], 16 * (NCH // 2))

            @block.vector
            def _(dve):
                def wide(at_):
                    return row(at_).unsqueeze(1).broadcast_to([P, CH, D])

                def link(c, k, ins):
                    ins.then_inc(prep.sem, 1)
                    prep.wait(dve, c, k)

                def gat_sums(c, s, n):
                    dve.wait_ge(ac_in[s], 16 * (n + 1))
                    aj = AC[s]
                    link(c, 1, nc.vector.tensor_scalar(rden, aj[:, :, D:MW], 1e-16, None, ALU.max))
                    link(c, 2, nc.vector.reciprocal(rden, rden))
                    for t in range(CH):
                        ins = nc.vector.tensor_tensor(O[:, t].rearrange("p (h c) -> p h c", h=HEADS),
                                                      aj[:, t, 0:D].rearrange("p (h c) -> p h c", h=HEADS),
                                                      rden[:, t].unsqueeze(2).broadcast_to([P, HEADS, D // HEADS]), ALU.mult)
                    link(c, 3, ins)
                    link(c, 4, nc.vector.tensor_tensor(O, O, wide(R_BIAS), ALU.add))
                    for t in range(CH):
                        ins = nc.vector.bn_stats(cst[:, 0, t], O[:, t])
                    link(c, 5, ins)

                def gat_norm(c):
                    pass_on(dve, "dve")
                    for t in range(CH):
                        ins = nc.vector.bn_aggr(cmv[:, 0, t], cst[:, 0, t])
                    link(c, 6, ins)
                    rsqrt(dve, c_rs, c, 0, crs[:, 0], cmv[:, 0, :, 1], ctv[:, 0], ctt[:, 0], LN_EPS)
                    for t in range(CH):
                        ins = nc.vector.tensor_scalar(O[:, t], O[:, t], cmv[:, 0, t, 0:1], crs[:, 0, t:t + 1],
                                                      ALU.subtract, ALU.mult)
                    link(c, 7, ins)

                def gat_scale(c):
                    link(c, 8, nc.vector.tensor_tensor(O, O, wide(R_GAMMA), ALU.mult))
                    link(c, 9, nc.vector.tensor_tensor(O, O, wide(R_BETA), ALU.add))
                    xf_tr.wait(dve, c - 1)
                    for t in range(CH):
                        ins = nc.vector.scalar_tensor_tensor(XF[:, t], O[:, t], 0.0, row(R_PRELU), ALU.min, ALU.mult)
                    link(c, 10, ins)

                def branches(c, s, n):
                    dve.wait_ge(y_in[s], 16 * (n + 1))
                    of, yf, xf = (v.rearrange("p t d -> p (t d)") for v in (O, Y[s], XF))
                    link(c, 11, nc.vector.scalar_tensor_tensor(yf, of, 0.0, yf, ALU.max, ALU.add))
                    link(c, 12, nc.vector.tensor_tensor(yf, yf, xf, ALU.add))
                    for t in range(CH):
                        ins = nc.vector.bn_stats(cst[:, 1, t], Y[s][:, t])
                    link(c, 13, ins)

                def second_norm(c, s):
                    pass_on(dve, "dve")
                    for t in range(CH):
                        ins = nc.vector.bn_aggr(cmv[:, 1, t], cst[:, 1, t])
                    link(c, 14, ins)
                    rsqrt(dve, c_rs, c, RSQ, crs[:, 1], cmv[:, 1, :, 1], ctv[:, 1], ctt[:, 1], LN_EPS)
                    for t in range(CH):
                        ins = nc.vector.tensor_scalar(XF[:, t], Y[s][:, t], cmv[:, 1, t, 0:1], crs[:, 1, t:t + 1],
                                                      ALU.subtract, ALU.mult)
                    ins.then_inc(xf_norm.sem, 1)

                def router_logits(c):
                    lg_mm.wait(dve, c)
                    br = rows[:, R_BR:R_BR + NEXP].unsqueeze(1).broadcast_to([P, CH, NEXP])
                    nc.vector.tensor_tensor(lg, ps[7][:, 0:CH * NEXP].rearrange("p (t e) -> p t e", t=CH), br,
                                            ALU.add).then_inc(lg_st.sem, 1)
                    lg_st.wait(dve, c, 1)
                    nc.vector.tensor_reduce(mx, lg, AX.X, ALU.max).then_inc(lg_st.sem, 1)
                    lg_st.wait(dve, c, 2)
                    nc.vector.tensor_tensor(lg, lg, mx.unsqueeze(2).broadcast_to([P, CH, NEXP]),
                                            ALU.subtract).then_inc(lg_sub.sem, 1)

                def router_weights(c, s):
                    ex_act.wait(dve, c)
                    nc.vector.tensor_reduce(sm, ex, AX.X, ALU.add).then_inc(lg_st.sem, 1)
                    lg_st.wait(dve, c, 3)
                    nc.vector.reciprocal(sm, sm).then_inc(lg_st.sem, 1)
                    lg_st.wait(dve, c, 4)
                    nc.vector.tensor_tensor(WT8[s], ex, sm.unsqueeze(2).broadcast_to([P, CH, NEXP]),
                                            ALU.mult).then_inc(w_set.sem, 1)

                def expert(c, s, e):
                    for t in range(CH):
                        if t % 2 == 0:
                            o2_mm.wait(dve, c, 2 * e + t // 2 + 1)
                            if e:
                                y_acc.wait(dve, c, e)
                        ins = nc.vector.scalar_tensor_tensor(Y[s][:, t], ps[4 + t // 2][:, (t % 2) * D:(t % 2 + 1) * D],
                                                             WT8[s][:, t, e:e + 1], Y[s][:, t], ALU.mult, ALU.add)
                    ins.then_inc(y_acc.sem, 1)

                def low_a(c, e):
                    for m in range(KD):
                        a_ev.wait(dve, c, 2 * e + m + 1)
                        nc.vector.tensor_tensor(ALO[e % 2][:, m], AR[:, m], AHI[e % 2][:, m].bitcast(f32),
                                                ALU.subtract).then_inc(a_lo.sem, 1)

                def low_b(c, e):
                    for m in range(KD):
                        b_ev.wait(dve, c, 2 * e + m + 1)
                        nc.vector.tensor_tensor(BLO[e % 2][:, m], BR[:, m], BHI[e % 2][:, m].bitcast(f32),
                                                ALU.subtract).then_inc(b_lo.sem, 1)

                def low_x(c, s):
                    xf_ev.wait(dve, c)
                    nc.vector.tensor_tensor(flat(XLO[s]), flat(XFR), flat(XHI[s]).bitcast(f32),
                                            ALU.subtract).then_inc(xf_lo.sem, 1)

                steps = [lambda: gat_sums(0, 0, 0), lambda: gat_norm(0), lambda: gat_scale(0),
                         lambda: branches(0, 0, 0), lambda: second_norm(0, 0)]
                for i, (w, lo) in enumerate(pieces):
                    if i % 2 == 0 and i // 2 < len(steps):
                        steps[i // 2]()
                    dve.wait_ge(w_hi, i + 1)
                    nc.vector.tensor_tensor(WLO[w][:, lo:lo + WP], WR[i % 2][:, :], WHI[w][:, lo:lo + WP].bitcast(f32),
                                            ALU.subtract).then_inc(w_lo, 1)
                low_x(0, 0)
                router_logits(0)
                router_weights(0, 0)
                low_a(0, 0)

                def body(c, s, n, last):
                    for e in range(NEXP):
                        if e == 6 and not last:
                            low_x(c + 1, 1 - s)
                        if e < NEXP - 1:
                            low_a(c, e + 1)
                        elif not last:
                            low_a(c + 1, 0)
                        if e == 0 and not (isinstance(c, int) and c == 0):
                            expert(c - 1, 1 - s, NEXP - 1)
                        low_b(c, e)
                        if e == 0:
                            bo_mm.wait(dve, c)
                            for j in range(2):
                                yj = Y[s][:, 2 * j:2 * j + 2].rearrange("p t d -> p (t d)")
                                ins = nc.vector.tensor_tensor(yj, yj, ps[6 + j][:, :], ALU.add)
                            ins.then_inc(y_init.sem, 1)
                            y_init.wait(dve, c)
                        else:
                            expert(c, s, e - 1)
                        if last:
                            continue
                        if e == 0:
                            gat_sums(c + 1, 1 - s, n + s)
                        if e == 1:
                            gat_norm(c + 1)
                        if e == 2:
                            gat_scale(c + 1)
                        if e == 3:
                            branches(c + 1, 1 - s, n + s)
                        if e == 4:
                            second_norm(c + 1, 1 - s)
                        if e == 6:
                            router_logits(c + 1)
                        if e == 7:
                            router_weights(c + 1, 1 - s)
                ring(dve, NCH, 2, body)
                expert(NCH - 1, (NCH - 1) % 2, NEXP - 1)

            @block.scalar
            def _(act):
                def layer_1(c, e):
                    for m in range(KD):
                        a_mm.wait(act, c, 2 * e + m + 1)
                        if e:
                            a_lo.wait(act, c, 2 * e + m - 1)
                        else:
                            a_lo.wait(act, c - 1, 2 * NEXP + m - 1)
                        i = 2 * e + m
                        nc.scalar.activation(AR[:, m], ps[m][:, :], ACT.Relu, scale=bn[:, i:i + 1],
                                             bias=bn[:, 16 + i:17 + i])
                        nc.scalar.activation(AHI[e % 2][:, m], ps[m][:, :], ACT.Relu, scale=bn[:, i:i + 1],
                                             bias=bn[:, 16 + i:17 + i]).then_inc(a_ev.sem, 1)

                def layer_2(c, e):
                    for m in range(KD):
                        b_mm.wait(act, c, 2 * e + m + 1)
                        if e:
                            b_lo.wait(act, c, 2 * e + m - 1)
                        else:
                            b_lo.wait(act, c - 1, 2 * NEXP + m - 1)
                        i = 2 * e + m
                        nc.scalar.activation(BR[:, m], ps[2 + m][:, :], ACT.Relu, scale=bn[:, 32 + i:33 + i],
                                             bias=bn[:, 48 + i:49 + i])
                        nc.scalar.activation(BHI[e % 2][:, m], ps[2 + m][:, :], ACT.Relu, scale=bn[:, 32 + i:33 + i],
                                             bias=bn[:, 48 + i:49 + i]).then_inc(b_ev.sem, 1)

                def xf_out(c, s):
                    xf_lo.wait(act, c - 1)
                    lg_mm.wait(act, c - 1)
                    for k in range(KD):
                        xf_tr.wait(act, c, k + 1)
                        nc.scalar.activation(XFR[:, k], ps[6 + k][:, :], ACT.Copy)
                        nc.scalar.activation(XHI[s][:, k], ps[6 + k][:, :], ACT.Copy).then_inc(xf_ev.sem, 1)

                for i, (w, lo) in enumerate(pieces):
                    act.wait_ge(wr_in[i % 2], 16 * (i // 2 + 1))
                    nc.scalar.activation(WHI[w][:, lo:lo + WP], WR[i % 2][:, :], ACT.Copy).then_inc(w_hi, 1)

                def router_exp(c):
                    lg_sub.wait(act, c)
                    nc.scalar.activation(ex, lg, ACT.Exp).then_inc(ex_act.sem, 1)

                xf_out(0, 0)
                router_exp(0)
                layer_1(0, 0)

                def body(c, s, n, last):
                    for e in range(NEXP):
                        if e < NEXP - 1:
                            layer_1(c, e + 1)
                        elif not last:
                            layer_1(c + 1, 0)
                        if e == 0:
                            w_tr.wait(act, c)
                            nc.scalar.activation(wT, ps[6][0:NEXP, :], ACT.Copy).then_inc(w_ev.sem, 1)
                        layer_2(c, e)
                        if e == 5 and not last:
                            xf_out(c + 1, 1 - s)
                        if e == 7 and not last:
                            router_exp(c + 1)
                ring(act, NCH, 2, body)

            @block.tensor
            def _(pe):
                def product(o, x, y, first, last):
                    nc.tensor.matmul(o, x[0], y[0], start=first, stop=False)
                    nc.tensor.matmul(o, x[0], y[1], start=False, stop=False)
                    return nc.tensor.matmul(o, x[1], y[0], start=False, stop=last)

                def weight_parts(i, e, k, cut):
                    at_ = (2 * e + k) * D
                    return [w[i][:, at_ + cut.start:at_ + cut.stop] for w in (WHI, WLO)]

                def layer_1(c, s, e):
                    if e == 0:
                        xf_lo.wait(pe, c)
                        a_ev.wait(pe, c - 1)
                    else:
                        a_ev.wait(pe, c, 2 * e)
                    for m in range(KD):
                        for k in range(KD):
                            ins = product(ps[m][:, :], weight_parts(0, e, k, slice(m * P, (m + 1) * P)),
                                          (XHI[s][:, k], XLO[s][:, k]), k == 0, k == KD - 1)
                        ins.then_inc(a_mm.sem, 1)

                def layer_2(c, e):
                    a_lo.wait(pe, c, 2 * e + 2)
                    if e:
                        b_ev.wait(pe, c, 2 * e)
                    else:
                        b_ev.wait(pe, c - 1)
                    for m in range(KD):
                        for k in range(KD):
                            ins = product(ps[2 + m][:, :], weight_parts(1, e, k, slice(m * P, (m + 1) * P)),
                                          (AHI[e % 2][:, k], ALO[e % 2][:, k]), k == 0, k == KD - 1)
                        ins.then_inc(b_mm.sem, 1)

                def layer_3(c, e):
                    b_lo.wait(pe, c, 2 * e + 2)
                    if e:
                        y_acc.wait(pe, c, e)
                    else:
                        y_acc.wait(pe, c - 1)
                    for t in range(CH):
                        for k in range(KD):
                            tile = slice(t * P, (t + 1) * P)
                            ins = product(ps[4 + t // 2][:, (t % 2) * D:(t % 2 + 1) * D],
                                          (BHI[e % 2][:, k, tile], BLO[e % 2][:, k, tile]),
                                          weight_parts(2, e, k, slice(0, D)), k == 0, k == KD - 1)
                        if t % 2:
                            ins.then_inc(o2_mm.sem, 1)

                def xf_transpose(c):
                    xf_norm.wait(pe, c)
                    y_init.wait(pe, c - 1)
                    for k in range(KD):
                        for t in range(CH):
                            ins = nc.tensor.transpose(ps[6 + k][:, t * P:(t + 1) * P], XF[:, t, k * P:(k + 1) * P],
                                                      ident[:, :])
                        ins.then_inc(xf_tr.sem, 1)

                def router(c, s):
                    xf_ev.wait(pe, c)
                    for t in range(CH):
                        for k in range(KD):
                            ins = nc.tensor.matmul(ps[7][:, t * NEXP:(t + 1) * NEXP], XFR[:, k, t * P:(t + 1) * P],
                                                   wr[:, k, :], start=k == 0, stop=k == KD - 1)
                    ins.then_inc(lg_mm.sem, 1)

                xf_transpose(0)
                router(0, 0)
                pe.wait_ge(w_lo, len(pieces))
                layer_1(0, 0, 0)

                def body(c, s, n, last):
                    for e in range(NEXP):
                        if e < NEXP - 1:
                            layer_1(c, s, e + 1)
                        elif not last:
                            layer_1(c + 1, 1 - s, 0)
                        if e == 0:
                            w_set.wait(pe, c)
                            for t in range(CH):
                                ins = nc.tensor.transpose(ps[6][0:NEXP, t * P:(t + 1) * P], WT8[s][:, t], ident[:, :])
                            ins.then_inc(w_tr.sem, 1)
                            if not (isinstance(c, int) and c == 0):
                                layer_3(c - 1, NEXP - 1)
                        layer_2(c, e)
                        if e == 0:
                            w_ev.wait(pe, c)
                            for t in range(CH):
                                ins = nc.tensor.matmul(ps[6 + t // 2][:, (t % 2) * D:(t % 2 + 1) * D],
                                                       wT[:, t * P:(t + 1) * P], bo[:, :], start=True, stop=True)
                            ins.then_inc(bo_mm.sem, 1)
                        else:
                            layer_3(c, e - 1)
                        if e == 5 and not last:
                            xf_transpose(c + 1)
                        if e == 6 and not last:
                            router(c + 1, 1 - s)
                ring(pe, NCH, 2, body)
                layer_3(NCH - 1, NEXP - 1)


_WEIGHTS = ["L0_gnn_W_src", "L0_gnn_W_dst", "L0_mix_Wq", "L0_mix_Wk", "L0_mix_Wv", "L0_mix_Wm", "L0_mix_W1", "L0_mix_W2",
            "L0_ffn_Wr", "L0_ffn_W1", "L0_ffn_W2", "L0_ffn_Wo", "L0_ffn_bo"]


def kernel(**inputs):
    import concourse.bacc as _bacc
    from concourse import mybir as _mybir
    from concourse.bass_utils import run_bass_kernel_spmd as _run

    g = {k: np.asarray(v) for k, v in inputs.items()}
    N, E = g["x"].shape[0], g["src"].shape[0]
    NP = -(-N // CT) * CT
    EP = -(-E // (P * GB)) * P * GB
    TE = EP // P
    KC = -(-TE // P)
    arrays = {name: np.ascontiguousarray(g[name]) for name in _WEIGHTS}
    arrays["x"] = np.concatenate([g["x"], np.zeros((NP - N, D), np.float32)])
    arrays["src"] = np.concatenate([g["src"], np.zeros(EP - E, np.int32)])
    dst = np.concatenate([g["dst"], np.full(EP - E, NP - 1, np.int32)])
    arrays["dst"] = dst
    edge = np.full(1, -1, np.int32)
    arrays["dst_prev"] = np.concatenate([edge, dst[:-1]])
    arrays["dst_next"] = np.concatenate([dst[1:], edge])
    ends = np.concatenate([dst.reshape(TE, P)[:, -1], np.full(KC * P - TE, 1 << 20, np.int32)])
    arrays["last_dst"] = np.ascontiguousarray(ends.reshape(KC, P).T)
    rows = [g["L0_gnn_bias"], g["L0_gnn_ln_gamma"], g["L0_gnn_ln_beta"], g["L0_gnn_prelu_w"], g["L0_mix_g2"], g["L0_mix_b2"],
            g["L0_ffn_br"], g["L0_gnn_att_src"].reshape(-1), g["L0_gnn_att_dst"].reshape(-1)]
    arrays["rows"] = np.ascontiguousarray(np.broadcast_to(np.concatenate(rows), (P, R_END)))
    cols = [g["L0_ffn_" + q].reshape(NEXP * KD, P) for q in ("b1", "g1", "be1", "m1", "v1", "b2", "g2", "be2", "m2", "v2")]
    cols += [g["L0_mix_g1"].reshape(KD, P), g["L0_mix_b1"].reshape(KD, P)]
    arrays["cols"] = np.ascontiguousarray(np.concatenate(cols).T)

    nc = _bacc.Bacc("TRN2", target_bir_lowering=False, num_devices=1)
    aps = {name: nc.dram_tensor("in_" + name, v.shape, _mybir.dt.from_np(v.dtype), kind="ExternalInput").ap()
           for name, v in arrays.items()}
    out = nc.dram_tensor("out_x", (NP, D), _mybir.dt.float32, kind="ExternalOutput").ap()
    build(nc, aps, out, N, E)
    r = _run(nc, [{"in_" + name: v for name, v in arrays.items()}], core_ids=[0])
    return r.results[0]["out_x"][:N]
```
